# Optimizing a Trainium2 kernel written in Bass

```python
import numpy as np
import jax
import jax.numpy as jnp

def _softmax(x, axis=-1):
    return jax.nn.softmax(x, axis=axis)

def _gelu(x):
    return jax.nn.gelu(x, approximate=True)

def _silu(x):
    return jax.nn.silu(x)

def _sigmoid(x):
    return jax.nn.sigmoid(x)

def _layernorm(x, axis=-1, eps=1e-05):
    m = jnp.mean(x, axis=axis, keepdims=True)
    v = jnp.var(x, axis=axis, keepdims=True)
    return (x - m) / jnp.sqrt(v + eps)

def _scatter_add(tgt, idx, src, axis=0):
    return tgt.at[idx].add(src)

def _segment_sum(src, seg, n):
    return jax.ops.segment_sum(src, seg, n)
kernel_name = 'mk_xattn_ffn_d4_seqx_r8_a53082'

def setup_inputs(seed: int=0):
    np.random.seed(seed)
    _w = jnp.asarray

    def _rec_inputs():
        import jax
        import jax.numpy as jnp
        _rk = jax.random.key(seed)
        x = -0.000125 + 0.9999 * jax.random.normal(jax.random.fold_in(_rk, 1), (8, 128, 512), jnp.float32)
        _lenS = 128 - jax.random.randint(jax.random.fold_in(_rk, 7), (8,), 0, max(1, 128 // 4) + 1, jnp.int32)
        _lenS2 = 128 - jax.random.randint(jax.random.fold_in(_rk, 8), (8,), 0, max(1, 128 // 4) + 1, jnp.int32)
        _ctx_4096P = jax.random.normal(jax.random.fold_in(_rk, 11), (8, 16, 512), jnp.float32)
        _ctx_4096c = jax.random.dirichlet(jax.random.fold_in(_rk, 511), 0.3 * jnp.ones((16,), jnp.float32), (8, 128))
        _ctx_4096t = jnp.einsum('bsk,bkd->bsd', _ctx_4096c, _ctx_4096P)
        _ctx_4096t = _ctx_4096t * jax.lax.rsqrt(jnp.mean(jnp.square(_ctx_4096t)) + 1e-12) * 0.953939
        ctx_4096 = -1.52775e-05 + 0.999936 * (_ctx_4096t + 0.3 * jax.random.normal(jax.random.fold_in(_rk, 611), (8, 128, 512), jnp.float32))
        return (x, ctx_4096)
    x, ctx_4096 = _rec_inputs()

    def _L0_xattn_setup():
        import jax, jax.numpy as jnp
        import numpy as np
        H = 8
        C = 2

        def _autocorrelation(Q, K, V):
            B, L, D = Q.shape
            d = D // H
            q = Q.reshape(B, L, H, d).transpose(0, 2, 1, 3)
            k = K.reshape(B, L, H, d).transpose(0, 2, 1, 3)
            v = V.reshape(B, L, H, d).transpose(0, 2, 1, 3)
            qf = jnp.fft.fft(q, axis=2)
            kf = jnp.fft.fft(k, axis=2)
            corr = jnp.fft.ifft(qf * jnp.conj(kf), axis=2).real
            topk = int(C * np.log(L))
            w, idx = jax.lax.top_k(corr.transpose(0, 1, 3, 2), topk)
            w = jax.nn.softmax(w, axis=-1)
            pos = jnp.arange(L)[:, None]
            out = jnp.zeros_like(v)
            for i in range(topk):
                g = jnp.minimum(idx[:, :, None, :, i] + pos, L - 1)
                out = out + w[:, :, None, :, i] * jnp.take_along_axis(v, g, axis=2)
            return out.transpose(0, 2, 1, 3).reshape(B, L, D)
        key = jax.random.key(seed)
        k1, k2, k3 = jax.random.split(key, 3)
        B, L, D = (16, 64, 512)
        Q = jax.random.normal(k1, (B, L, D), dtype=jnp.float32)
        K = jax.random.normal(k2, (B, L, D), dtype=jnp.float32)
        V = jax.random.normal(k3, (B, L, D), dtype=jnp.float32)
        return {'Q': Q, 'K': K, 'V': V}
    _L0_xattn_all = _L0_xattn_setup()
    _L0_xattn_in = {k: v for k, v in _L0_xattn_all.items() if k in ()}
    del _L0_xattn_all

    def _L0_ffn_setup():
        import jax, jax.numpy as jnp
        import numpy as np
        BITS = 8

        def _quantize(w, bits=BITS):
            n = float(2 ** (bits - 1) - 1)
            scale = jnp.max(jnp.abs(w)) / n
            wq = jnp.clip(jnp.round(w / scale), -n, n) * scale
            return wq
        key = jax.random.key(seed)
        k1, k2, k3 = jax.random.split(key, 3)
        B, S, IN, OUT = (4, 256, 512, 512)
        x = jax.random.normal(k1, (B, S, IN), dtype=jnp.float32)
        weight = jax.random.normal(k2, (OUT, IN), dtype=jnp.float32)
        bias = jax.random.normal(k3, (OUT,), dtype=jnp.float32)
        return {'x': x, 'weight': weight, 'bias': bias}
    _L0_ffn_all = _L0_ffn_setup()
    _L0_ffn_in = {k: v for k, v in _L0_ffn_all.items() if k in ('weight', 'bias')}
    del _L0_ffn_all

    def _L1_xattn_setup():
        import jax, jax.numpy as jnp
        import numpy as np
        HID = 512
        NHEAD = 32
        NKV = 8
        HDIM = 128
        G = NHEAD // NKV
        key = jax.random.key(seed)
        ks = jax.random.split(key, 6)
        s = 0.02
        B, L = (2, 256)
        return {'query': jax.random.normal(ks[0], (B, L, HID), jnp.float32), 'kv': jax.random.normal(ks[1], (B, L, HID), jnp.float32), 'Wq': jax.random.normal(ks[2], (HID, NHEAD * HDIM), jnp.float32) * s, 'bq': jnp.zeros((NHEAD * HDIM,), jnp.float32), 'Wkv': jax.random.normal(ks[3], (HID, 2 * NKV * HDIM), jnp.float32) * s, 'bkv': jnp.zeros((2 * NKV * HDIM,), jnp.float32), 'Wo': jax.random.normal(ks[4], (NHEAD * HDIM, HID), jnp.float32) * s, 'bo': jnp.zeros((HID,), jnp.float32)}
    _L1_xattn_all = _L1_xattn_setup()
    _L1_xattn_in = {k: v for k, v in _L1_xattn_all.items() if k in ('Wq', 'bq', 'Wkv', 'bkv', 'Wo', 'bo')}
    del _L1_xattn_all

    def _L1_ffn_setup():
        import jax, jax.numpy as jnp
        import numpy as np
        B, S, D, O, E, R = (4, 256, 512, 512, 8, 16)
        SCALING = 32.0 / 16.0
        MAX_THRESHOLD = 0.125
        key = jax.random.key(seed)
        ks = jax.random.split(key, 8)
        return {'x': jax.random.normal(ks[0], (B, S, D), jnp.float32), 'W_base': jax.random.normal(ks[1], (O, D), jnp.float32) * (1.0 / np.sqrt(D)), 'b_base': jax.random.normal(ks[2], (O,), jnp.float32) * 0.02, 'W_gate': jax.random.normal(ks[3], (E, D), jnp.float32) * (1.0 / np.sqrt(D)), 'W_thr': jax.random.normal(ks[4], (D,), jnp.float32) * (1.0 / np.sqrt(D)), 'b_thr': jax.random.normal(ks[5], (1,), jnp.float32) * 0.02, 'A_w': jax.random.normal(ks[6], (E, R, D), jnp.float32) * (1.0 / np.sqrt(D)), 'B_w': jax.random.normal(ks[7], (E, O, R), jnp.float32) * (1.0 / np.sqrt(R))}
    _L1_ffn_all = _L1_ffn_setup()
    _L1_ffn_in = {k: v for k, v in _L1_ffn_all.items() if k in ('W_base', 'b_base', 'W_gate', 'W_thr', 'b_thr', 'A_w', 'B_w')}
    del _L1_ffn_all

    def _L2_xattn_setup():
        import jax, jax.numpy as jnp
        import numpy as np
        B, C, D = (8, 128, 512)
        GROUPS = 8
        ATTN_SCALE = 1.0
        RESID = 1.0
        EPS = 1e-05
        key = jax.random.key(seed)
        ks = jax.random.split(key, 9)
        s = 1.0 / np.sqrt(C)
        return {'inp_q': jax.random.normal(ks[0], (B, C, D), jnp.float32), 'inp_k': jax.random.normal(ks[1], (B, C, D), jnp.float32), 'inp_v': jax.random.normal(ks[2], (B, C, D), jnp.float32), 'Wt': jax.random.normal(ks[3], (C, C), jnp.float32) * s, 'Wp': jax.random.normal(ks[4], (C, C), jnp.float32) * s, 'Wg': jax.random.normal(ks[5], (C, C), jnp.float32) * s, 'Wz': jax.random.normal(ks[6], (C, C // GROUPS), jnp.float32) * s, 'gn_w': jax.random.normal(ks[7], (C,), jnp.float32), 'gn_b': jax.random.normal(ks[8], (C,), jnp.float32)}
    _L2_xattn_all = _L2_xattn_setup()
    _L2_xattn_in = {k: v for k, v in _L2_xattn_all.items() if k in ('Wt', 'Wp', 'Wg', 'Wz', 'gn_w', 'gn_b')}
    del _L2_xattn_all

    def _L2_ffn_setup():
        import jax, jax.numpy as jnp
        import numpy as np
        B, L, H, Dh, M = (4, 256, 16, 32, 128)
        D = H * Dh
        key = jax.random.key(seed)
        kx, ku, kd, kp = jax.random.split(key, 4)
        x = jax.random.normal(kx, (B, L, D), dtype=jnp.float32)
        up = jax.random.normal(ku, (H, Dh, M), dtype=jnp.float32)
        down = jax.random.normal(kd, (H, M, Dh), dtype=jnp.float32)
        perm = jax.random.permutation(kp, D)
        return {'x': x, 'up': up, 'down': down, 'perm': perm}
    _L2_ffn_all = _L2_ffn_setup()
    _L2_ffn_in = {k: v for k, v in _L2_ffn_all.items() if k in ('up', 'down', 'perm')}
    del _L2_ffn_all

    def _L3_xattn_setup():
        import jax, jax.numpy as jnp
        import numpy as np
        EMB_DIM = 512
        NHEADS = 32
        KVHEADS = 8
        HEAD_DIM = 128
        ROPE_BASE = 10000.0

        def _rope(x):
            B, H, S, D = x.shape
            inv_freq = 1.0 / ROPE_BASE ** (jnp.arange(0, D, 2, dtype=jnp.float32) / D)
            ang = jnp.arange(S, dtype=jnp.float32)[:, None] * inv_freq[None, :]
            cos = jnp.concatenate([jnp.cos(ang), jnp.cos(ang)], axis=-1)
            sin = jnp.concatenate([jnp.sin(ang), jnp.sin(ang)], axis=-1)
            x1, x2 = (x[..., :D // 2], x[..., D // 2:])
            rot = jnp.concatenate([-x2, x1], axis=-1)
            return x * cos + rot * sin
        key = jax.random.key(seed)
        ks = jax.random.split(key, 7)
        B, S = (2, 256)
        std_qk = EMB_DIM ** (-0.5)
        std_vd = (1.0 / (EMB_DIM * NHEADS * HEAD_DIM) ** 0.5) ** 0.5
        return {'q': jax.random.normal(ks[0], (B, S, EMB_DIM), jnp.float32), 'k': jax.random.normal(ks[1], (B, S, EMB_DIM), jnp.float32), 'v': jax.random.normal(ks[2], (B, S, EMB_DIM), jnp.float32), 'Wq': jax.random.normal(ks[3], (NHEADS * HEAD_DIM, EMB_DIM), jnp.float32) * std_qk, 'Wk': jax.random.normal(ks[4], (KVHEADS * HEAD_DIM, EMB_DIM), jnp.float32) * std_qk, 'Wv': jax.random.normal(ks[5], (KVHEADS * HEAD_DIM, EMB_DIM), jnp.float32) * std_vd, 'Wd': jax.random.normal(ks[6], (EMB_DIM, NHEADS * HEAD_DIM), jnp.float32) * std_vd}
    _L3_xattn_all = _L3_xattn_setup()
    _L3_xattn_in = {k: v for k, v in _L3_xattn_all.items() if k in ('Wq', 'Wk', 'Wv', 'Wd')}
    del _L3_xattn_all

    def _L3_ffn_setup():
        import jax, jax.numpy as jnp
        import numpy as np
        NF4_CODE = jnp.array([-1.0, -0.6961928009986877, -0.5250730514526367, -0.39491748809814453, -0.28444138169288635, -0.18477343022823334, -0.09105003625154495, 0.0, 0.07958029955625534, 0.16093020141124725, 0.24611230194568634, 0.33791524171829224, 0.44070982933044434, 0.5626170039176941, 0.7229568362236023, 1.0], dtype=jnp.float32)
        BLOCKSIZE = 64

        def nf4_quant_dequant(w):
            shape = w.shape
            flat = w.reshape(-1, BLOCKSIZE)
            absmax = jnp.max(jnp.abs(flat), axis=1, keepdims=True)
            normalized = flat / jnp.where(absmax == 0, 1.0, absmax)
            bounds = (NF4_CODE[:-1] + NF4_CODE[1:]) * 0.5
            idx = jnp.searchsorted(bounds, normalized)
            return (NF4_CODE[idx] * absmax).reshape(shape)
        key = jax.random.key(seed)
        k1, k2, k3, kx = jax.random.split(key, 4)
        D, H = (512, 1376)
        scale = 0.02
        w1 = jax.random.normal(k1, (H, D), jnp.float32) * scale
        w2 = jax.random.normal(k2, (H, D), jnp.float32) * scale
        w3 = jax.random.normal(k3, (D, H), jnp.float32) * scale
        x = jax.random.normal(kx, (2, 256, D), jnp.float32)
        return {'x': x, 'w1': w1, 'w2': w2, 'w3': w3}
    _L3_ffn_all = _L3_ffn_setup()
    _L3_ffn_in = {k: v for k, v in _L3_ffn_all.items() if k in ('w1', 'w2', 'w3')}
    del _L3_ffn_all
    return {'x': x, 'ctx_4096': ctx_4096, 'L0_ffn_weight': _L0_ffn_in['weight'], 'L0_ffn_bias': _L0_ffn_in['bias'], 'L1_xattn_Wq': _L1_xattn_in['Wq'], 'L1_xattn_bq': _L1_xattn_in['bq'], 'L1_xattn_Wkv': _L1_xattn_in['Wkv'], 'L1_xattn_bkv': _L1_xattn_in['bkv'], 'L1_xattn_Wo': _L1_xattn_in['Wo'], 'L1_xattn_bo': _L1_xattn_in['bo'], 'L1_ffn_W_base': _L1_ffn_in['W_base'], 'L1_ffn_b_base': _L1_ffn_in['b_base'], 'L1_ffn_W_gate': _L1_ffn_in['W_gate'], 'L1_ffn_W_thr': _L1_ffn_in['W_thr'], 'L1_ffn_b_thr': _L1_ffn_in['b_thr'], 'L1_ffn_A_w': _L1_ffn_in['A_w'], 'L1_ffn_B_w': _L1_ffn_in['B_w'], 'L2_xattn_Wt': _L2_xattn_in['Wt'], 'L2_xattn_Wp': _L2_xattn_in['Wp'], 'L2_xattn_Wg': _L2_xattn_in['Wg'], 'L2_xattn_Wz': _L2_xattn_in['Wz'], 'L2_xattn_gn_w': _L2_xattn_in['gn_w'], 'L2_xattn_gn_b': _L2_xattn_in['gn_b'], 'L2_ffn_up': _L2_ffn_in['up'], 'L2_ffn_down': _L2_ffn_in['down'], 'L2_ffn_perm': _L2_ffn_in['perm'], 'L3_xattn_Wq': _L3_xattn_in['Wq'], 'L3_xattn_Wk': _L3_xattn_in['Wk'], 'L3_xattn_Wv': _L3_xattn_in['Wv'], 'L3_xattn_Wd': _L3_xattn_in['Wd'], 'L3_ffn_w1': _L3_ffn_in['w1'], 'L3_ffn_w2': _L3_ffn_in['w2'], 'L3_ffn_w3': _L3_ffn_in['w3']}

def reference(x, ctx_4096, L0_ffn_weight, L0_ffn_bias, L1_xattn_Wq, L1_xattn_bq, L1_xattn_Wkv, L1_xattn_bkv, L1_xattn_Wo, L1_xattn_bo, L1_ffn_W_base, L1_ffn_b_base, L1_ffn_W_gate, L1_ffn_W_thr, L1_ffn_b_thr, L1_ffn_A_w, L1_ffn_B_w, L2_xattn_Wt, L2_xattn_Wp, L2_xattn_Wg, L2_xattn_Wz, L2_xattn_gn_w, L2_xattn_gn_b, L2_ffn_up, L2_ffn_down, L2_ffn_perm, L3_xattn_Wq, L3_xattn_Wk, L3_xattn_Wv, L3_xattn_Wd, L3_ffn_w1, L3_ffn_w2, L3_ffn_w3):
    import jax
    import jax.numpy as jnp

    def _L0_xattn_ref(Q, K, V):
        import jax, jax.numpy as jnp
        import numpy as np
        H = 8
        C = 2

        def _autocorrelation(Q, K, V):
            B, L, D = Q.shape
            d = D // H
            q = Q.reshape(B, L, H, d).transpose(0, 2, 1, 3)
            k = K.reshape(B, L, H, d).transpose(0, 2, 1, 3)
            v = V.reshape(B, L, H, d).transpose(0, 2, 1, 3)
            qf = jnp.fft.fft(q, axis=2)
            kf = jnp.fft.fft(k, axis=2)
            corr = jnp.fft.ifft(qf * jnp.conj(kf), axis=2).real
            topk = int(C * np.log(L))
            w, idx = jax.lax.top_k(corr.transpose(0, 1, 3, 2), topk)
            w = jax.nn.softmax(w, axis=-1)
            pos = jnp.arange(L)[:, None]
            out = jnp.zeros_like(v)
            for i in range(topk):
                g = jnp.minimum(idx[:, :, None, :, i] + pos, L - 1)
                out = out + w[:, :, None, :, i] * jnp.take_along_axis(v, g, axis=2)
            return out.transpose(0, 2, 1, 3).reshape(B, L, D)
        return _autocorrelation(Q, K, V)

    def _L0_ffn_ref(x, weight, bias):
        import jax, jax.numpy as jnp
        import numpy as np
        BITS = 8

        def _quantize(w, bits=BITS):
            n = float(2 ** (bits - 1) - 1)
            scale = jnp.max(jnp.abs(w)) / n
            wq = jnp.clip(jnp.round(w / scale), -n, n) * scale
            return wq
        wq = _quantize(weight)
        y = jnp.einsum('bsi,oi->bso', x, wq)
        return y + bias

    def _L1_xattn_ref(query, kv, Wq, bq, Wkv, bkv, Wo, bo):
        import jax, jax.numpy as jnp
        import numpy as np
        HID = 512
        NHEAD = 32
        NKV = 8
        HDIM = 128
        G = NHEAD // NKV
        B, L, _ = query.shape
        Lk = kv.shape[1]
        scale = jnp.asarray(1.0 / np.sqrt(HDIM), query.dtype)
        q = (query @ Wq + bq).reshape(B, L, NKV, G, HDIM)
        k_, v_ = jnp.split(kv @ Wkv + bkv, 2, axis=-1)
        k = k_.reshape(B, Lk, NKV, HDIM)
        v = v_.reshape(B, Lk, NKV, HDIM)
        scores = jnp.einsum('blkgd,bmkd->bkglm', q, k) * scale
        attn = jax.nn.softmax(scores, axis=-1)
        o = jnp.einsum('bkglm,bmkd->blkgd', attn, v).reshape(B, L, NHEAD * HDIM)
        return o @ Wo + bo

    def _L1_ffn_ref(x, W_base, b_base, W_gate, W_thr, b_thr, A_w, B_w):
        import jax, jax.numpy as jnp
        import numpy as np
        B, S, D, O, E, R = (4, 256, 512, 512, 8, 16)
        SCALING = 32.0 / 16.0
        MAX_THRESHOLD = 0.125
        base = jnp.einsum('bsd,od->bso', x, W_base) + b_base
        xf = x.reshape(-1, D)
        gate = jax.nn.softmax(xf @ W_gate.T, axis=-1)
        thr = jax.nn.sigmoid(xf @ W_thr + b_thr[0]) * MAX_THRESHOLD
        adapted = gate - thr[:, None]
        selected = (adapted >= 0).astype(x.dtype)
        w = adapted * selected
        wsum = jnp.sum(w, axis=-1, keepdims=True)
        wsum = jnp.where(wsum == 0, jnp.ones_like(wsum), wsum)
        w = w / wsum
        h = jnp.einsum('nd,erd->ner', xf, A_w)
        moe = jnp.einsum('ner,ne,eor->no', h, w, B_w) * SCALING
        return base + moe.reshape(base.shape)

    def _L2_xattn_ref(inp_q, inp_k, inp_v, Wt, Wp, Wg, Wz, gn_w, gn_b):
        import jax, jax.numpy as jnp
        import numpy as np
        B, C, D = (8, 128, 512)
        GROUPS = 8
        ATTN_SCALE = 1.0
        RESID = 1.0
        EPS = 1e-05
        residual = inp_v * RESID
        t = jnp.einsum('oc,bcd->bod', Wt, inp_v)
        p = jnp.einsum('oc,bcd->bod', Wp, inp_q)
        g = jnp.einsum('oc,bcd->bod', Wg, inp_k)
        b, c, d = t.shape
        cg = c // GROUPS
        tg = t.reshape(b, GROUPS, cg * d)
        pg = p.reshape(b, GROUPS, cg * d)
        gg = g.reshape(b, GROUPS, cg * d)
        att = jnp.sum(pg * gg, axis=-1, keepdims=True) * ATTN_SCALE
        x = (att * tg).reshape(b, c, d)
        xg = x.reshape(b, GROUPS, cg, d)
        Wzg = Wz.reshape(GROUPS, cg, cg)
        y = jnp.einsum('goi,bgid->bgod', Wzg, xg).reshape(b, c, d)
        yg = y.reshape(b, GROUPS, cg * d)
        mu = jnp.mean(yg, axis=-1, keepdims=True)
        var = jnp.var(yg, axis=-1, keepdims=True)
        yn = ((yg - mu) * jax.lax.rsqrt(var + EPS)).reshape(b, c, d)
        return yn * gn_w[None, :, None] + gn_b[None, :, None] + residual

    def _L2_ffn_ref(x, up, down, perm):
        import jax, jax.numpy as jnp
        import numpy as np
        B, L, H, Dh, M = (4, 256, 16, 32, 128)
        D = H * Dh
        b, l, Dm = x.shape
        h, d = (up.shape[0], up.shape[1])
        unperm = jnp.argsort(perm)
        t = x.reshape(b * l, Dm)
        t = t[:, perm]
        t = t.reshape(b * l, h, d)
        t = jnp.einsum('bhd,hdm->bhm', t, up)
        t = jax.nn.gelu(t, approximate=False)
        t = jnp.einsum('bhm,hmd->bhd', t, down)
        t = t.reshape(b * l, h * d)
        t = t[:, unperm]
        out = t.reshape(b, l, Dm)
        return out

    def _L3_xattn_ref(q, k, v, Wq, Wk, Wv, Wd):
        import jax, jax.numpy as jnp
        import numpy as np
        EMB_DIM = 512
        NHEADS = 32
        KVHEADS = 8
        HEAD_DIM = 128
        ROPE_BASE = 10000.0

        def _rope(x):
            B, H, S, D = x.shape
            inv_freq = 1.0 / ROPE_BASE ** (jnp.arange(0, D, 2, dtype=jnp.float32) / D)
            ang = jnp.arange(S, dtype=jnp.float32)[:, None] * inv_freq[None, :]
            cos = jnp.concatenate([jnp.cos(ang), jnp.cos(ang)], axis=-1)
            sin = jnp.concatenate([jnp.sin(ang), jnp.sin(ang)], axis=-1)
            x1, x2 = (x[..., :D // 2], x[..., D // 2:])
            rot = jnp.concatenate([-x2, x1], axis=-1)
            return x * cos + rot * sin
        B, Sq, _ = q.shape
        Skv = k.shape[1]
        queries = (q @ Wq.T).reshape(B, Sq, NHEADS, HEAD_DIM).transpose(0, 2, 1, 3)
        keys = (k @ Wk.T).reshape(B, Skv, KVHEADS, HEAD_DIM).transpose(0, 2, 1, 3)
        values = (v @ Wv.T).reshape(B, Skv, KVHEADS, HEAD_DIM).transpose(0, 2, 1, 3)
        queries = _rope(queries)
        keys = _rope(keys)
        exp = NHEADS // KVHEADS
        keys = jnp.repeat(keys, exp, axis=1)
        values = jnp.repeat(values, exp, axis=1)
        scale = HEAD_DIM ** (-0.5)
        scores = jnp.einsum('bhqd,bhkd->bhqk', queries, keys) * scale
        causal = jnp.tril(jnp.ones((Sq, Skv), dtype=bool))
        scores = jnp.where(causal[None, None], scores, jnp.finfo(scores.dtype).min)
        attn = jax.nn.softmax(scores, axis=-1)
        ctx = jnp.einsum('bhqk,bhkd->bhqd', attn, values)
        ctx = ctx.transpose(0, 2, 1, 3).reshape(B, Sq, NHEADS * HEAD_DIM)
        return ctx @ Wd.T

    def _L3_ffn_ref(x, w1, w2, w3):
        import jax, jax.numpy as jnp
        import numpy as np
        NF4_CODE = jnp.array([-1.0, -0.6961928009986877, -0.5250730514526367, -0.39491748809814453, -0.28444138169288635, -0.18477343022823334, -0.09105003625154495, 0.0, 0.07958029955625534, 0.16093020141124725, 0.24611230194568634, 0.33791524171829224, 0.44070982933044434, 0.5626170039176941, 0.7229568362236023, 1.0], dtype=jnp.float32)
        BLOCKSIZE = 64

        def nf4_quant_dequant(w):
            shape = w.shape
            flat = w.reshape(-1, BLOCKSIZE)
            absmax = jnp.max(jnp.abs(flat), axis=1, keepdims=True)
            normalized = flat / jnp.where(absmax == 0, 1.0, absmax)
            bounds = (NF4_CODE[:-1] + NF4_CODE[1:]) * 0.5
            idx = jnp.searchsorted(bounds, normalized)
            return (NF4_CODE[idx] * absmax).reshape(shape)
        dq1 = nf4_quant_dequant(w1)
        dq2 = nf4_quant_dequant(w2)
        dq3 = nf4_quant_dequant(w3)
        gate = jnp.einsum('bsd,hd->bsh', x, dq1)
        up = jnp.einsum('bsd,hd->bsh', x, dq2)
        h = jax.nn.silu(gate) * up
        return jnp.einsum('bsh,dh->bsd', h, dq3)
    x = x + _L0_xattn_ref(_layernorm(x, axis=-1), ctx_4096, ctx_4096)
    x = x + _L0_ffn_ref(_layernorm(x, axis=-1), L0_ffn_weight, L0_ffn_bias)
    x = x + _L1_xattn_ref(_layernorm(x, axis=-1), ctx_4096, L1_xattn_Wq, L1_xattn_bq, L1_xattn_Wkv, L1_xattn_bkv, L1_xattn_Wo, L1_xattn_bo)
    x = x + _L1_ffn_ref(_layernorm(x, axis=-1), L1_ffn_W_base, L1_ffn_b_base, L1_ffn_W_gate, L1_ffn_W_thr, L1_ffn_b_thr, L1_ffn_A_w, L1_ffn_B_w)
    x = x + _L2_xattn_ref(_layernorm(x, axis=-1), ctx_4096, ctx_4096, L2_xattn_Wt, L2_xattn_Wp, L2_xattn_Wg, L2_xattn_Wz, L2_xattn_gn_w, L2_xattn_gn_b)
    x = x + _L2_ffn_ref(_layernorm(x, axis=-1), L2_ffn_up, L2_ffn_down, L2_ffn_perm)
    x = x + _L3_xattn_ref(_layernorm(x, axis=-1), ctx_4096, ctx_4096, L3_xattn_Wq, L3_xattn_Wk, L3_xattn_Wv, L3_xattn_Wd)
    x = x + _L3_ffn_ref(_layernorm(x, axis=-1), L3_ffn_w1, L3_ffn_w2, L3_ffn_w3)
    return x

_drawn_inputs = setup_inputs


def setup_inputs(seed=0):
    import zlib

    import numpy as np

    out = dict(_drawn_inputs(seed))
    spreads = {'L1_xattn_bq': (0.0, 0.8), 'L1_xattn_bkv': (0.0, 0.8), 'L1_xattn_bo': (0.0, 0.8)}
    factors = {'L1_xattn_Wq': 8.0,
     'L1_xattn_Wkv': 4.595,
     'L1_xattn_Wo': 3.917,
     'L1_ffn_b_base': 22.725,
     'L1_ffn_W_thr': 8.0,
     'L2_xattn_gn_b': 2.791,
     'L3_xattn_Wq': 8.0,
     'L3_xattn_Wk': 8.0,
     'L3_xattn_Wv': 5.081,
     'L3_xattn_Wd': 4.978,
     'L3_ffn_w1': 8.0,
     'L3_ffn_w2': 8.0,
     'L3_ffn_w3': 8.0}
    for name, (base, spread) in spreads.items():
        noise = np.random.default_rng([zlib.crc32(name.encode()), seed]).standard_normal(out[name].shape)
        drawn = base * np.exp(spread * noise) if base else spread * noise
        out[name] = jnp.asarray(drawn.astype(out[name].dtype))
    for name, factor in factors.items():
        out[name] = (out[name] * factor).astype(out[name].dtype)
    return out
```

```python
from contextlib import ExitStack

import numpy as np
import concourse.bass as bass
from concourse import mybir

ALU = mybir.AluOpType
ACT = mybir.ActivationFunctionType
AX = mybir.AxisListType
F32, F32R, I32 = mybir.dt.float32, mybir.dt.float32r, mybir.dt.int32
P = 128
D = 512
K_CH = D // P
N_BATCH = 8
HEAD_DIM = 128
N_KV = 8
GROUP = 4
HIDDEN = 1376
CODE_TILES = 35
EPS = 1e-5


class Steps:

    def __init__(self, sem, names):
        self.sem, self.names, self.at = sem, list(names), 0

    def done(self, instruction, name):
        assert self.names[self.at % len(self.names)] == name, (self.names[self.at % len(self.names)], name)
        self.at += 1
        instruction.then_inc(self.sem, 1)

    def value(self, name, k):
        return k * len(self.names) + (self.names.index(name) + 1)


def both(stage, *more):
    return [(s, j) for j in (0, 1) for s in (stage, *more)]


def hi_lo(t, *index):
    return [t[(slice(None), a) + index] for a in (0, 1)]


def product(pe, out, lhs, rhs, first=True, last=True):
    terms = [(a, b) for l, r in zip(lhs, rhs) for n, a in enumerate(l) for m, b in enumerate(r) if n + m < 2]
    for t, (a, b) in enumerate(terms):
        i = pe.matmul(out, a, b, start=first and t == 0, stop=last and t == len(terms) - 1)
    return i


def inverse_root(dve, y, v, t, iterations=3):
    dve.tensor_scalar(y.bitcast(I32), v.bitcast(I32), -0.5, float(0x5F3759DF), ALU.mult, ALU.add)
    dve.drain()
    for _ in range(iterations):
        dve.tensor_tensor(t, y, y, ALU.mult)
        dve.drain()
        dve.scalar_tensor_tensor(t, t, -0.5, v, ALU.mult, ALU.mult)
        dve.drain()
        dve.scalar_tensor_tensor(y, t, 1.5, y, ALU.add, ALU.mult)
        dve.drain()


class Norm:

    def __init__(self, sb, name):
        self.stats = sb(name + "_stats", [P, 2, 6])
        self.mv = sb(name + "_mean_var", [P, 2, 2])
        self.var, self.rstd, self.tmp = (sb(name + x, [P, 2]) for x in ("_var", "_rstd", "_tmp"))

    def emit(self, dve, xs, outs, said):
        for j in (0, 1):
            dve.bn_stats(self.stats[:, j], xs[j])
        dve.drain()
        for j in (0, 1):
            dve.bn_aggr(self.mv[:, j], self.stats[:, j])
        dve.drain()
        dve.tensor_scalar(self.var[:], self.mv[:, :, 1], EPS, None, ALU.add)
        dve.drain()
        inverse_root(dve, self.rstd[:], self.var[:], self.tmp[:])
        for j in (0, 1):
            said(dve.tensor_scalar(outs[j], xs[j], self.mv[:, j, 0:1], self.rstd[:, j:j + 1], ALU.subtract, ALU.mult), j)


def dft_matrices():
    L = 128
    n = np.arange(L)
    k = np.concatenate([np.arange(65), np.arange(1, 64)])
    imag = np.arange(L) >= 65
    ang = 2 * np.pi * np.outer(n, k) / L
    c, s = np.cos(ang), np.sin(ang)
    qa, qb = np.where(imag, -s, c), np.where(imag, c, s)
    va, vb = c.copy(), s.copy()
    va[L - 1, 0] += L
    sign = np.where(imag, -1.0, 1.0)
    weight = np.where((k == 0) | (k == 64), 1.0, 2.0)
    basis = np.where(imag, s, c).T
    icorr = basis * (weight * sign / L)[:, None]
    ieven = basis * (weight / (2 * L))[:, None]
    j = 2 * np.concatenate([np.arange(64), np.arange(64)]) + 1
    imag = np.arange(L) >= 64
    ang = 2 * np.pi * np.outer(n, j) / (2 * L)
    c, s = np.cos(ang), np.sin(ang)
    woa, wob = np.where(imag, -s, c), np.where(imag, c, s)
    voa, vob = c.copy(), s.copy()
    voa[L - 1] -= c.sum(0)
    vob[L - 1] -= s.sum(0)
    iodd = np.where(imag, s, c).T * (2.0 / (2 * L))
    mats = [qa, qb, va, vb, voa, vob, woa, wob, icorr, ieven, iodd]
    return np.ascontiguousarray(np.stack(mats, 1).astype(np.float32))


NF4_CODE = [-1.0, -0.6961928009986877, -0.5250730514526367, -0.39491748809814453, -0.28444138169288635,
            -0.18477343022823334, -0.09105003625154495, 0.0, 0.07958029955625534, 0.16093020141124725,
            0.24611230194568634, 0.33791524171829224, 0.44070982933044434, 0.5626170039176941, 0.7229568362236023, 1.0]


class CodeTiles:
    BLOCK = 64

    def __init__(self, nc, stack, name, codes, apart, worker, first, per_pass, passes):
        self.src, self.dst = codes
        self.on_pool = worker == "pool"
        self.first, self.per_pass, self.total = first, per_pass, per_pass * passes
        sb = lambda n, shape: stack.enter_context(nc.sbuf_tensor(name + n, shape, F32))
        sem = lambda n: stack.enter_context(nc.semaphore(name + n))
        nb = D // self.BLOCK
        self.v, self.u = sb("v", [P, nb, self.BLOCK]), sb("u", [P, nb, self.BLOCK])
        if self.on_pool:
            self.step = sb("step", [P, nb, self.BLOCK])
        self.absmax, self.inv = sb("absmax", [P, nb]), sb("inv", [P, nb])
        self.s_in, self.s_scaled, self.s_coded, self.s_out = (sem(n) for n in ("in", "scaled", "coded", "out"))
        self.apart = apart
        code = np.array(NF4_CODE, np.float32)
        self.bounds = [float(b) for b in (code[:-1] + code[1:]) * np.float32(0.5)]
        self.rises = [float(r) for r in code[1:] - code[:-1]]
        self.queues = {}

    def _wide(self, t):
        return t[:].unsqueeze(2).broadcast_to([P, D // self.BLOCK, self.BLOCK])

    def _rows(self, t, n):
        rows = t[bass.ds((n + self.first) * P, P)] if not isinstance(n, int) else t[(n + self.first) * P:(n + self.first + 1) * P]
        return rows.rearrange("p (n b) -> p n b", b=self.BLOCK)

    def _load(self, sp, n):
        sp.dma_start(self.v[:], self._rows(self.src, n)).then_inc(self.s_in, 16)

    def start(self, sp):
        sp.sem_inc(self.s_out, 1)
        self._load(sp, 0)

    def turn(self, sp, k, i):
        n = k * self.per_pass + i
        sp.wait_ge(self.s_coded, n + 1)
        sp.dma_start(self._rows(self.dst, n), self.u[:]).then_inc(self.s_out, 16)
        self._load(sp, n + 1)

    def finish(self, sp):
        sp.wait_ge(self.s_out, 16 * self.total + 1)
        sp.wait_ge(self.s_in, 16 * (self.total + 1))

    def _wait(self, eng, s, value):
        eng.wait_ge(s, value)
        if not isinstance(value, int):
            eng.sem_inc(self.apart, 1)

    def _scale(self, dve, n):
        def part_1():
            self._wait(dve, self.s_in, 16 * (n + 1))
            dve.tensor_reduce(self.absmax[:], self.v[:], AX.X, ALU.max, apply_absolute_value=True)
            dve.drain()
            dve.tensor_scalar(self.inv[:], self.absmax[:], 0.0, None, ALU.is_equal)
            dve.drain()
            dve.tensor_tensor(self.inv[:], self.absmax[:], self.inv[:], ALU.add)
            dve.drain()
            dve.reciprocal(self.inv[:], self.inv[:])
            dve.drain()

        def part_2():
            dve.tensor_tensor(self.v[:], self.v[:], self._wide(self.inv), ALU.mult).then_inc(self.s_scaled, 1)

        return [part_1, part_2]

    def _code(self, eng, n):
        def first():
            self._wait(eng, self.s_scaled, n + 1)
            self._wait(eng, self.s_out, 16 * n + 1)
            eng.tensor_scalar(self.u[:], self.v[:], self.bounds[14], self.rises[14], ALU.is_gt, ALU.mult)
            eng.drain()

        def rise(r):
            eng.tensor_scalar(self.u[:], self.u[:], r, None, ALU.add)
            eng.drain()

        def bracket(b):
            eng.scalar_tensor_tensor(self.u[:], self.v[:], b, self.u[:], ALU.is_gt, ALU.mult)
            eng.drain()

        def step(b, r):
            eng.tensor_scalar(self.step[:], self.v[:], b, r, ALU.is_gt, ALU.mult)
            eng.drain()

        def add():
            eng.tensor_tensor(self.u[:], self.u[:], self.step[:], ALU.add)
            eng.drain()

        def minus_one():
            eng.tensor_scalar(self.u[:], self.u[:], 1.0, -1.0, ALU.mult, ALU.add)
            eng.drain()

        def unscale():
            eng.tensor_tensor(self.u[:], self.u[:], self._wide(self.absmax), ALU.mult).then_inc(self.s_coded, 1)

        def last():
            eng.scalar_tensor_tensor(self.u[:], self.u[:], -1.0, self._wide(self.absmax), ALU.add, ALU.mult).then_inc(self.s_coded, 1)

        ops = [first]
        if self.on_pool:
            for r, b in zip(self.rises[13::-1], self.bounds[13::-1]):
                ops += [lambda r=r, b=b: step(b, r), add]
            return ops + [minus_one, unscale]
        for r, b in zip(self.rises[13::-1], self.bounds[13::-1]):
            ops += [lambda r=r: rise(r), lambda b=b: bracket(b)]
        return ops + [last]

    def begin(self, eng, k, scale=False, code=False):
        ops = []
        for i in range(self.per_pass):
            n = k * self.per_pass + i
            ops += (self._scale(eng, n) if scale else []) + (self._code(eng, n) if code else [])
        self.queues[id(eng)] = ops

    def fill(self, eng, steps=10 ** 6):
        ops = self.queues.get(id(eng), [])
        while ops and steps:
            ops.pop(0)()
            steps -= 1


def fill(streams, eng, steps=10 ** 6):
    for stream in streams.values():
        stream.fill(eng, steps)


def begin(streams, eng, worker, k):
    for who, stream in streams.items():
        stream.begin(eng, k, scale=worker == "dve", code=who == worker)


def turn(streams, sp, k, begin=0, end=6):
    for sixth in range(begin, end):
        for stream in streams.values():
            for i in range(stream.per_pass):
                if (6 * (i + 1) - 1) // stream.per_pass == sixth:
                    stream.turn(sp, k, i)


def correlation_and_quantized_ffn(nc, resid, xnT, w, codes, tiles):
    NAMES = ["qa", "qb", "va", "vb", "voa", "vob", "woa", "wob", "icorr", "ieven", "iodd"]
    with ExitStack() as stack:
        sb = lambda name, shape, dt=F32: stack.enter_context(nc.sbuf_tensor("a_" + name, shape, dt))
        sem = lambda name: stack.enter_context(nc.semaphore("a_" + name))
        raw_dft = sb("raw_dft", [P, len(NAMES), P])
        dft = sb("dft", [P, 2, len(NAMES), P], F32R)
        raw_w8 = sb("raw_w8", [P, K_CH, D])
        w8 = sb("w8", [P, K_CH, D], F32R)
        bias8 = sb("bias8", [P, D])
        ident = sb("ident", [P, P])
        ones = sb("ones", [P, P])
        wmax, wmax_all, w8_scale, w8_inv = sb("wmax", [P, 1]), sb("wmax_all", [P, 1]), sb("w8_scale", [P, 1]), sb("w8_inv", [P, 1])
        x_in, ctx_in = sb("x_in", [P, 2, D]), sb("ctx_in", [P, 2, D])
        xn = sb("xn", [P, 2, D])
        xs, cs = sb("xs", [P, 2, 2, D], F32R), sb("cs", [P, 2, 2, D], F32R)
        spec = sb("spec", [P, 2, 4, D])
        t1, t2, tsum = sb("t1", [P, 2, D]), sb("t2", [P, 2, D]), sb("tsum", [P, 2, D])
        prod = sb("prod", [P, 2, 2, D], F32R)
        top8, next8 = sb("top8", [P, 4, 8]), sb("next8", [P, 4, 8])
        ninth = sb("ninth", [P, 4, 8])
        cut, cut2 = sb("cut", [P, 4, P + 8]), sb("cut2", [P, 4, P + 8])
        neg = sb("neg", [P, 2, 4])
        e_lag = sb("e_lag", [P, 2, 4, P])
        wsum, wrec = sb("wsum", [P, 4]), sb("wrec", [P, 4])
        wT = sb("wT", [P, 2, 2, D], F32R)
        x1, x1b, x2 = sb("x1", [P, 2, D]), sb("x1b", [P, 2, D]), sb("x2", [P, 2, D])
        xT = sb("xT", [P, 2, 2, K_CH, P], F32R)
        norm = Norm(sb, "norm")
        ps = stack.enter_context(nc.psum_tensor("a_ps", [P, 8, 512], F32))

        TAKEN, SENTINEL = -3.0e38, -2.0e38
        idx = {n: i for i, n in enumerate(NAMES)}
        mat = lambda n: [dft[:, a, idx[n]] for a in (0, 1)]

        s_const, s_setup, s_bc = sem("const"), sem("setup"), sem("bc")
        s_x, s_ctx, apart = sem("x"), sem("ctx"), sem("apart")
        SPEC = ("va", "vb", "voa", "vob")
        pe_s = Steps(sem("pe"), [(n, j) for j in (0, 1) for n in (*SPEC, "q")] + both("corr") + both("wT")
                     + [(n, j) for j in (0, 1) for n in ("we", "wo")] + both("out") + both("xT") + both("y") + both("xnT"))
        act_s = Steps(sem("act"), both("cs") + both("xs") + [(n, j) for j in (0, 1) for n in SPEC] + both("prod") + both("exp")
                      + both("wT") + [(n, j) for j in (0, 1) for n in ("we", "wo")] + both("xT") + both("xnT"))
        dve_s = Steps(sem("dve"), both("xn") + both("prod") + [(n, j) for j in (0, 1) for n in ("neg", "w")] + both("wT")
                      + [(n, j) for j in (0, 1) for n in ("we", "wo")] + both("x1") + both("xn2") + both("xT") + both("x2")
                      + both("xn3") + both("resid") + both("xnT"))
        pool_s = Steps(sem("pool"), both("cs") + both("xs") + [(n, j) for j in (0, 1) for n in ("psum", "plow")]
                       + [(n, j) for j in (0, 1) for n in ("we", "welow", "wo", "wolow")] + both("x1b"))
        steps = {"pe": pe_s, "act": act_s, "dve": dve_s, "pool": pool_s}

        def wait_for(eng, k, *names, apart_for=False):
            for who, name, j in names:
                eng.wait_ge(steps[who].sem, steps[who].value((name, j), k))
            if apart_for and not isinstance(k, int):
                eng.sem_inc(apart, 1)

        waits = wait_for

        def waits_before(eng, k, *names):
            for who, name, j in names:
                s = steps[who]
                v = s.value((name, j), k) - len(s.names)
                if isinstance(v, int) and v <= 0:
                    continue
                eng.wait_ge(s.sem, v)

        PAIRS = N_BATCH // 2
        streams = {who: CodeTiles(nc, stack, "a_n_" + who, codes, apart, who, *tile, PAIRS) for who, tile in tiles.items()}
        block = stack.enter_context(nc.Block())

        def loop(eng, emit):
            emit(0)
            with eng.Fori(1, PAIRS) as k:
                emit(k)

        @block.sync
        def _(sp):
            for dst, src in ((raw_dft, w["dft"]), (raw_w8, w["w8"]), (ident, w["ident"]), (bias8, w["bias8"].broadcast_to([P, D]))):
                sp.dma_start(dst[:], src).then_inc(s_const, 16)

            def emit(k):
                waits_before(sp, k, ("dve", "x1", 1))
                sp.dma_start(x_in[:], w["x"][bass.ds(2 * k, 2)].rearrange("b p d -> p b d")).then_inc(s_x, 16)
                waits_before(sp, k, ("act", "cs", 1), ("pool", "cs", 1))
                sp.dma_start(ctx_in[:], w["ctx"][bass.ds(2 * k, 2)].rearrange("b p d -> p b d")).then_inc(s_ctx, 16)
                turn(streams, sp, k)
            for st in streams.values():
                st.start(sp)
            loop(sp, emit)
            for st in streams.values():
                st.finish(sp)

        @block.gpsimd
        def _(pool):
            pool.wait_ge(s_const, 64)
            pool.tensor_scalar(dft[:, 0], raw_dft[:], 1.0, 0.0, ALU.mult, ALU.add)
            pool.drain()
            pool.tensor_tensor(dft[:, 1], raw_dft[:], dft[:, 0], ALU.subtract).then_inc(s_setup, 1)

            def emit(k):
                begin(streams, pool, "pool", k)
                for j in (0, 1):
                    waits(pool, k, ("act", "cs", j))
                    pool_s.done(pool.tensor_tensor(cs[:, 1, j], ctx_in[:, j], cs[:, 0, j], ALU.subtract), ("cs", j))
                for j in (0, 1):
                    waits(pool, k, ("act", "xs", j))
                    pool_s.done(pool.tensor_tensor(xs[:, 1, j], xn[:, j], xs[:, 0, j], ALU.subtract), ("xs", j))
                for j in (0, 1):
                    waits(pool, k, ("dve", "prod", j))
                    pool_s.done(pool.tensor_tensor(tsum[:, j], t1[:, j], t2[:, j], ALU.add), ("psum", j))
                    waits(pool, k, ("act", "prod", j))
                    pool_s.done(pool.tensor_tensor(prod[:, 1, j], tsum[:, j], prod[:, 0, j], ALU.subtract), ("plow", j))
                fill(streams, pool, 16)
                for j in (0, 1):
                    for n, part in (("we", 0), ("wo", 1)):
                        waits(pool, k, ("dve", n, j))
                        pool_s.done(pool.tensor_tensor(tsum[:, part], t1[:, part], t2[:, part], ALU.add), (n, j))
                        waits(pool, k, ("act", n, j))
                        pool_s.done(pool.tensor_tensor(prod[:, 1, part], tsum[:, part], prod[:, 0, part], ALU.subtract), (n + "low", j))
                for j in (0, 1):
                    waits(pool, k, ("dve", "x1", j))
                    pool_s.done(pool.tensor_tensor(x1b[:, j], x1[:, j], bias8[:], ALU.add), ("x1b", j))
                fill(streams, pool)
            loop(pool, emit)

        @block.tensor
        def _(pe):
            pe.wait_ge(s_const, 64)
            pe.wait_ge(s_bc, 1)
            pe.transpose(ps[0:1, 6, 0:P], wmax[:], ident[:]).then_inc(s_bc, 1)
            pe.wait_ge(s_bc, 3)
            pe.matmul(ps[:, 7, 0:1], ones[0:1, :], wmax_all[0:1, :], start=True, stop=True).then_inc(s_bc, 1)
            pe.wait_ge(s_bc, 5)
            pe.wait_ge(s_setup, 1)

            def emit(k):
                for j in (0, 1):
                    for b, n in enumerate(SPEC):
                        if b == 0:
                            waits(pe, k, ("pool", "cs", j))
                        if j == 0 and b in (0, 2):
                            waits_before(pe, k, ("dve", ("we", "we", "wo")[b], 1))
                        if j == 1:
                            waits(pe, k, ("act", n, 0))
                        pe_s.done(product(pe, ps[:, b], [mat(n)], [hi_lo(cs, j)]), (n, j))
                    waits(pe, k, ("pool", "xs", j))
                    if j == 0:
                        waits_before(pe, k, ("dve", "xnT", 1))
                    else:
                        waits(pe, k, ("dve", "prod", 0))
                    product(pe, ps[:, 4], [mat("qa")], [hi_lo(xs, j)])
                    pe_s.done(product(pe, ps[:, 5], [mat("qb")], [hi_lo(xs, j)]), ("q", j))
                for j in (0, 1):
                    waits(pe, k, ("pool", "plow", j))
                    if j == 0:
                        waits_before(pe, k, ("dve", "x2", 1))
                    for c in range(4):
                        i = product(pe, ps[:, 6 + j, c * P:(c + 1) * P], [hi_lo(prod, j, slice(c * P, (c + 1) * P))], [mat("icorr")])
                    pe_s.done(i, ("corr", j))
                for j in (0, 1):
                    waits(pe, k, ("dve", "w", j))
                    for c in range(4):
                        i = pe.transpose(ps[:, 4 + j, c * P:(c + 1) * P], e_lag[:, j, c], ident[:])
                    pe_s.done(i, ("wT", j))
                for j in (0, 1):
                    waits(pe, k, ("dve", "wT", j))
                    for b, n in enumerate(("qa", "qb", "woa", "wob")):
                        if j == 1:
                            waits(pe, k, ("dve", ("we", "we", "wo", "wo")[b], 0))
                        i = product(pe, ps[:, b], [mat(n)], [hi_lo(wT, j)])
                        if b % 2:
                            pe_s.done(i, (("we", "wo")[b // 2], j))
                for j in (0, 1):
                    waits(pe, k, ("pool", "wolow", j))
                    pe_s.done(product(pe, ps[:, 6 + j], [mat("ieven"), mat("iodd")], [hi_lo(prod, 0), hi_lo(prod, 1)]), ("out", j))
                for j in (0, 1):
                    waits(pe, k, ("dve", "xn2", j))
                    for c in range(4):
                        i = pe.transpose(ps[:, 4 + j, c * P:(c + 1) * P], xn[:, j, c * P:(c + 1) * P], ident[:])
                    pe_s.done(i, ("xT", j))
                for j in (0, 1):
                    waits(pe, k, ("dve", "xT", j))
                    pe_s.done(product(pe, ps[:, 6 + j], [hi_lo(xT, j, c) for c in range(K_CH)], [[w8[:, c]] for c in range(K_CH)]), ("y", j))
                for j in (0, 1):
                    waits(pe, k, ("dve", "xn3", j))
                    for c in range(4):
                        i = pe.transpose(ps[:, 4 + j, c * P:(c + 1) * P], xn[:, j, c * P:(c + 1) * P], ident[:])
                    pe_s.done(i, ("xnT", j))
            loop(pe, emit)

        @block.scalar
        def _(act):
            def emit(k):
                if isinstance(k, int):
                    act.wait_ge(s_ctx, 16)
                else:
                    act.wait_ge(s_ctx, k * 16 + 16)
                for j in (0, 1):
                    if j == 0:
                        waits_before(act, k, ("pe", "q", 1))
                    act_s.done(act.copy(cs[:, 0, j], ctx_in[:, j]), ("cs", j))
                for j in (0, 1):
                    waits(act, k, ("dve", "xn", j))
                    act_s.done(act.copy(xs[:, 0, j], xn[:, j]), ("xs", j))
                for j in (0, 1):
                    for b, n in enumerate(SPEC):
                        waits(act, k, ("pe", n, j))
                        act_s.done(act.copy(spec[:, j, b], ps[:, b]), (n, j))
                for j in (0, 1):
                    waits(act, k, ("pool", "psum", j))
                    act_s.done(act.copy(prod[:, 0, j], tsum[:, j]), ("prod", j))
                for j in (0, 1):
                    waits(act, k, ("dve", "neg", j))
                    for c in range(4):
                        i = act.activation(e_lag[:, j, c], ps[:, 6 + j, c * P:(c + 1) * P], ACT.Exp, bias=neg[:, j, c:c + 1])
                    act_s.done(i, ("exp", j))
                for j in (0, 1):
                    waits(act, k, ("pe", "wT", j))
                    act_s.done(act.copy(wT[:, 0, j], ps[:, 4 + j]), ("wT", j))
                for j in (0, 1):
                    for part, n in enumerate(("we", "wo")):
                        waits(act, k, ("pool", n, j))
                        if j == 1 and part == 0:
                            waits(act, k, ("pe", "out", 0))
                        act_s.done(act.copy(prod[:, 0, part], tsum[:, part]), (n, j))
                for j in (0, 1):
                    waits(act, k, ("pe", "xT", j))
                    act_s.done(act.copy(xT[:, 0, j], ps[:, 4 + j].rearrange("p (c t) -> p c t", c=K_CH)), ("xT", j))
                for j in (0, 1):
                    waits(act, k, ("pe", "xnT", j), apart_for=True)
                    dst = xnT[:, 0, :, bass.ds(2 * P * k + j * P, P)]
                    act_s.done(act.copy(dst, ps[:, 4 + j].rearrange("p (c t) -> p c t", c=K_CH)), ("xnT", j))
            loop(act, emit)

        @block.vector
        def _(dve):
            dve.memset(ones[:], 1.0)
            dve.memset(ninth[:], SENTINEL)
            dve.memset(cut[:], SENTINEL)
            dve.wait_ge(s_const, 64)
            dve.tensor_reduce(wmax[:], raw_w8[:], AX.XY, ALU.max, apply_absolute_value=True).then_inc(s_bc, 1)
            dve.wait_ge(s_bc, 2)
            dve.tensor_reduce(wmax_all[0:1, :], ps[0:1, 6, 0:P], AX.X, ALU.max).then_inc(s_bc, 1)
            dve.wait_ge(s_bc, 4)
            dve.tensor_scalar(w8_scale[:], ps[:, 7, 0:1], 1.0 / 127.0, None, ALU.mult)
            dve.drain()
            dve.reciprocal(w8_inv[:], w8_scale[:])
            dve.drain()
            ROUND = float(3 << 22)
            dve.tensor_scalar(raw_w8[:], raw_w8[:], w8_inv[:], ROUND, ALU.mult, ALU.add)
            dve.drain()
            dve.tensor_scalar(raw_w8[:], raw_w8[:], ROUND, 127.0, ALU.subtract, ALU.min)
            dve.drain()
            dve.tensor_scalar(w8[:], raw_w8[:], -127.0, None, ALU.max).then_inc(s_bc, 1)

            def waits(eng, k, *names, apart_for=False):
                fill(streams, dve, 2)
                wait_for(eng, k, *names, apart_for=apart_for)

            def emit(k):
                begin(streams, dve, "dve", k)
                dve.wait_ge(s_x, k * 16 + 16)
                norm.emit(dve, [x_in[:, j] for j in (0, 1)], [xn[:, j] for j in (0, 1)], lambda i, j: dve_s.done(i, ("xn", j)))
                for j in (0, 1):
                    waits(dve, k, ("pe", "q", j), ("act", "vb", j))
                    dve.tensor_tensor(t1[:, j], ps[:, 4], spec[:, j, 0], ALU.mult)
                    dve_s.done(dve.tensor_tensor(t2[:, j], ps[:, 5], spec[:, j, 1], ALU.mult), ("prod", j))
                for j in (0, 1):
                    waits(dve, k, ("pe", "corr", j), apart_for=True)
                    corr = lambda c: ps[:, 6 + j, c * P:(c + 1) * P]
                    for c in range(4):
                        dve.max(top8[:, c], corr(c))
                    dve.drain()
                    dve.tensor_scalar(neg[:, j], top8[:, :, 0], -1.0, None, ALU.mult)
                    for c in range(4):
                        i = dve.match_replace(cut[:, c, 0:P], top8[:, c], corr(c), TAKEN)
                    dve_s.done(i, ("neg", j))
                    dve.drain()
                    for c in range(4):
                        dve.max(next8[:, c], cut[:, c, 0:P])
                    dve.drain()
                    dve.tensor_copy(ninth[:, :, 0], next8[:, :, 0])
                    dve.drain()
                    for c in range(4):
                        dve.match_replace(cut2[:, c], ninth[:, c], cut[:, c], TAKEN)
                    dve.drain()
                    waits(dve, k, ("act", "exp", j))
                    dve.scalar_tensor_tensor(e_lag[:, j], cut2[:, :, 0:P], 0.5 * (TAKEN + SENTINEL), e_lag[:, j], ALU.is_le, ALU.mult)
                    dve.drain()
                    dve.tensor_reduce(wsum[:], e_lag[:, j], AX.X, ALU.add)
                    dve.drain()
                    dve.reciprocal(wrec[:], wsum[:])
                    dve.drain()
                    dve_s.done(dve.tensor_tensor(e_lag[:, j], e_lag[:, j], wrec[:].unsqueeze(2).broadcast_to([P, 4, P]), ALU.mult), ("w", j))
                for j in (0, 1):
                    waits(dve, k, ("act", "wT", j))
                    dve_s.done(dve.tensor_tensor(wT[:, 1, j], ps[:, 4 + j], wT[:, 0, j], ALU.subtract), ("wT", j))
                for j in (0, 1):
                    for part, n in enumerate(("we", "wo")):
                        waits(dve, k, ("pe", n, j))
                        if j == 1:
                            waits(dve, k, ("pool", n, 0))
                        elif part == 0:
                            waits(dve, k, ("act", "vob", 1))
                        dve.tensor_tensor(t1[:, part], ps[:, 2 * part], spec[:, j, 2 * part], ALU.mult)
                        dve_s.done(dve.tensor_tensor(t2[:, part], ps[:, 2 * part + 1], spec[:, j, 2 * part + 1], ALU.mult), (n, j))
                for j in (0, 1):
                    waits(dve, k, ("pe", "out", j))
                    dve_s.done(dve.tensor_tensor(x1[:, j], ps[:, 6 + j], x_in[:, j], ALU.add), ("x1", j))
                dve.drain()
                norm.emit(dve, [x1[:, j] for j in (0, 1)], [xn[:, j] for j in (0, 1)], lambda i, j: dve_s.done(i, ("xn2", j)))
                for j in (0, 1):
                    waits(dve, k, ("act", "xT", j))
                    dve_s.done(dve.tensor_tensor(xT[:, 1, j], ps[:, 4 + j].rearrange("p (c t) -> p c t", c=K_CH), xT[:, 0, j], ALU.subtract), ("xT", j))
                for j in (0, 1):
                    waits(dve, k, ("pe", "y", j), ("pool", "x1b", j))
                    dve_s.done(dve.scalar_tensor_tensor(x2[:, j], ps[:, 6 + j], w8_scale[:], x1b[:, j], ALU.mult, ALU.add), ("x2", j))
                dve.drain()
                norm.emit(dve, [x2[:, j] for j in (0, 1)], [xn[:, j] for j in (0, 1)], lambda i, j: dve_s.done(i, ("xn3", j)))
                for j in (0, 1):
                    dve_s.done(dve.tensor_copy(resid[:, bass.ds(2 * k + j, 1)].rearrange("p a d -> p (a d)"), x2[:, j]), ("resid", j))
                for j in (0, 1):
                    waits(dve, k, ("act", "xnT", j), apart_for=True)
                    sl = bass.ds(2 * P * k + j * P, P)
                    dve_s.done(dve.tensor_tensor(xnT[:, 1, :, sl], ps[:, 4 + j].rearrange("p (c t) -> p c t", c=K_CH), xnT[:, 0, :, sl], ALU.subtract), ("xnT", j))
                fill(streams, dve)
            loop(dve, emit)


def grouped_attention(nc, tag, resid, xnT, ctxT, ctxT_dram, w, tables, codes, tiles):
    rope = tables is not None
    biased = w.get("bq") is not None
    n_groups, n_heads = w["wq"].shape[0], w["wq"].shape[1]
    units = n_groups * N_BATCH
    scale = float(HEAD_DIM) ** -0.5
    HALF = 4
    TILE_STEPS = tiles["dve"][1] if "dve" in tiles else 0

    with ExitStack() as stack:
        sb = lambda name, shape, dt=F32: stack.enter_context(nc.sbuf_tensor(tag + name, shape, dt))
        ps = lambda name, shape: stack.enter_context(nc.psum_tensor(tag + name, shape, F32))
        sem = lambda name: stack.enter_context(nc.semaphore(tag + name))

        raw_q = sb("raw_q", [P, 2, K_CH, P])
        raw_k = sb("raw_k", [P, K_CH, P])
        raw_v = sb("raw_v", [P, K_CH, P])
        raw_o = sb("raw_o", [P, 2, D])
        wq = sb("wq", [P, 2, n_heads, K_CH, P], F32R)
        wk = sb("wk", [P, 2, K_CH, P], F32R)
        wv = sb("wv", [P, 2, K_CH, P], F32R)
        wo = sb("wo", [P, 2, 2, n_heads, D], F32R)
        qT = sb("qT", [P, 2, 2, n_heads, HALF, P], F32R)
        kT = sb("kT", [P, 2, 2, HALF, P], F32R)
        vv = sb("vv", [P, 2, 2, HALF, P], F32R)
        v_cols = sb("v_cols", [P, HALF, P])
        prob = sb("prob", [P, 2, n_heads, P])
        probT = sb("probT", [P, 2, n_heads, P], F32R)
        oT = sb("oT", [P, 2, n_heads, P], F32R)
        negmax = sb("negmax", [P, 2, n_heads])
        sums = sb("sums", [P, 2, n_heads])
        recip = sb("recip", [P, 2, n_heads])
        ident = sb("ident", [P, P])
        if biased:
            bq = sb("bq", [P, n_groups * n_heads])
            bk = sb("bk", [P, n_groups])
            bv = sb("bv", [P, n_groups])
            bo = sb("bo", [P, D])
        if rope:
            cosT = sb("cosT", [P, P])
            sinT = sb("sinT", [P, P])
            mask = sb("mask", [P, P])
            rot_a = sb("rot_a", [P, HALF, P])
            rot_b = sb("rot_b", [P, HALF, P])
            roped = sb("roped", [P, HALF, P])

        ps_job = ps("ps_job", [P, 2, 512])
        ps_s = ps("ps_s", [P, 2, n_heads, P])
        ps_t = ps("ps_t", [P, n_heads, P])
        ps_v = ps("ps_v", [P, n_heads, P])
        ps_o = ps("ps_o", [P, 2, 512])

        ctx_raw = [prob[:].rearrange("p a h m -> p (a h m)"), raw_o[:].rearrange("p a n -> p (a n)")]
        s_ctx, s_ctx_high, s_ctx_split = [sem("ctx0"), sem("ctx1")], sem("ctx_high"), sem("ctx_split")
        s_const = sem("const")
        s_rawq, s_rawo = [sem(f"rawq{j}") for j in (0, 1)], [sem(f"rawo{j}") for j in (0, 1)]
        s_rawk, s_rawv = sem("rawk"), sem("rawv")
        act_wq, act_wk, act_wv, act_wo = (sem("act_w" + x) for x in "qkvo")
        s_wq, s_wk, s_wv, s_wo = (sem("w" + x) for x in "qkvo")
        s_apart = sem("apart")
        s_xb = sem("xb")
        pe_s, pe_t, pe_q, pe_kv, pe_o, pe_pv = (sem("pe_" + x) for x in ("s", "t", "q", "kv", "o", "pv"))
        act_vt, pe_vt = sem("act_vt"), sem("pe_vt")
        act_t, act_e, act_q, act_kv, act_o = (sem("act_" + x) for x in ("t", "e", "q", "kv", "o"))
        dve_m, dve_t, dve_n, dve_q, dve_kv, dve_x, dve_o = (
            sem("dve_" + x) for x in ("m", "t", "n", "q", "kv", "x", "o"))
        s_rot, s_sum = sem("rot"), sem("sum")

        streams = {who: CodeTiles(nc, stack, tag + "n_" + who, codes, s_apart, who, *tile, n_groups - 2) for who, tile in tiles.items()}

        def schedule(eng, emit, worker=None):
            for n in range(-HALF, HALF):
                emit(n, 0)
            with eng.Fori(0, n_groups - 2) as k:
                if worker:
                    begin(streams, eng, worker, k)
                for c in range(HALF, HALF + N_BATCH):
                    emit(c, k)
                fill(streams, eng)
            for c in range(HALF, units + 2 - N_BATCH * (n_groups - 2)):
                emit(c, n_groups - 2)

        def unit(c, k):
            return k * N_BATCH + c if isinstance(k, int) else c

        def jobs_at(c, k):
            return unit(c, k) < units - HALF

        def next_weights_at(c, k):
            return c >= 0 and (c // HALF) % 2 == 0 and unit(c, k) < units - N_BATCH

        def next_output_at(c, k):
            return (c // HALF) % 2 == 1 and unit(c, k) < units - N_BATCH

        def wo_part(g, j):
            if isinstance(g, int):
                return lambda a: wo[:, g % 2, a, j]
            return lambda a: wo[:, bass.ds(g % 2, 1), a, j].rearrange("p a n -> p (a n)")

        def valid(c, k, lag):
            return 0 <= unit(c, k) - lag < units

        def count(c, k, lag=0):
            return k * N_BATCH + (c - lag + 1)

        def job_count(c, k):
            return k * N_BATCH + c + HALF + 1

        def kv_before(c, k):
            return k * 4 + 2 * (c // HALF + 1) + (0, 0, 1, 1)[c % HALF]

        def halves(c, k):
            return k * 2 + (c // HALF + 2)

        def rots_before(c, k):
            return k * 10 + 5 * (c // HALF + 1) + (0, 1, 3, 4)[c % HALF]

        n_const = 1 + (4 if biased else 0) + (3 if rope else 0)
        BANK_Q, BANK_K, BANK_V = (0, 1, 1, 0), 0, 1

        block = stack.enter_context(nc.Block())

        @block.sync
        def _(sp):
            def loads(g, tiles_pass=None):
                started = not isinstance(g, int) or g > 0
                group = lambda name: w[name][bass.ds(g, 1)]
                if not started:
                    sp.dma_start(raw_q[:, 0], w["wq"][0, 0]).then_inc(s_rawq[0], 16)
                    sp.dma_start(ctx_raw[0], ctxT_dram[:, 0]).then_inc(s_ctx[0], 16)
                    sp.dma_start(raw_q[:, 1], w["wq"][0, 1]).then_inc(s_rawq[1], 16)
                    sp.dma_start(raw_k[:], w["wk"][0]).then_inc(s_rawk, 16)
                    sp.dma_start(ctx_raw[1], ctxT_dram[:, 1]).then_inc(s_ctx[1], 16)
                    for dst, src in ([(ident, w["ident"])]
                                     + ([(bq, w["bq"]), (bk, w["bk"]), (bv, w["bv"]), (bo, w["bo"].broadcast_to([P, D]))] if biased else [])
                                     + ([(cosT, tables[0]), (sinT, tables[1]), (mask, tables[2])] if rope else [])):
                        sp.dma_start(dst[:], src).then_inc(s_const, 16)
                    for kc in (2, 3):
                        sp.wait_ge(s_ctx_split, kc - 1)
                        sp.dma_start(ctx_raw[kc % 2], ctxT_dram[:, kc]).then_inc(s_ctx[kc % 2], 16)
                for j in range(0 if started else 2, n_heads):
                    if j == 2 and tiles_pass is not None:
                        turn(streams, sp, tiles_pass, 0, 5)
                    if started or j >= 2:
                        sp.wait_ge(s_wq, g * 4 + (j - 1))
                    sp.dma_start(raw_q[:, j % 2], group("wq")[:, j].rearrange("a p k d -> (a p) k d")).then_inc(s_rawq[j % 2], 16)
                    if j == 1:
                        if started:
                            sp.wait_ge(s_wk, g)
                        sp.dma_start(raw_k[:], group("wk").rearrange("a p k d -> (a p) k d")).then_inc(s_rawk, 16)
                if started:
                    sp.wait_ge(s_wv, g)
                sp.dma_start(raw_v[:], group("wv").rearrange("a p k d -> (a p) k d")).then_inc(s_rawv, 16)
                if not started:
                    sp.wait_ge(s_ctx_split, K_CH)
                for j in range(n_heads):
                    if j == 2 and tiles_pass is not None:
                        turn(streams, sp, tiles_pass, 5, 6)
                    if started or j >= 2:
                        sp.wait_ge(s_wo, g * 4 + (j - 1))
                    sp.dma_start(raw_o[:, j % 2], group("wo")[:, j].rearrange("a d n -> (a d) n")).then_inc(s_rawo[j % 2], 16)

            loads(0)
            for st in streams.values():
                st.start(sp)
            loads(1)
            with sp.Fori(2, n_groups) as g:
                loads(g, g - 2)
            for st in streams.values():
                st.finish(sp)
            sp.wait_ge(s_const, 16 * n_const)

        @block.gpsimd
        def _(pool):
            def low(s_hi, value, part, raw, done):
                pool.wait_ge(s_hi, value)
                if not isinstance(value, int):
                    pool.sem_inc(s_apart, 1)
                pool.tensor_tensor(part(1), raw, part(0), ALU.subtract).then_inc(done, 1)

            def rope_sum(n_before, read, n_read):
                pool.wait_ge(s_rot, n_before + 1)
                pool.wait_ge(read, n_read)
                pool.tensor_tensor(roped[:], rot_a[:], rot_b[:], ALU.add).then_inc(s_sum, 1)

            if biased:
                pool.wait_ge(s_const, 16 * n_const)
                for b in range(N_BATCH):
                    i = pool.tensor_tensor(resid[:, b], resid[:, b], bo[:], ALU.add)
                i.then_inc(s_xb, 1)

            def emit(c, k):
                i = c % HALF
                if jobs_at(c, k) and rope:
                    r = rots_before(c, k)
                    if i == 2:
                        rope_sum(r, dve_kv, kv_before(c, k))
                    elif unit(c, k) > -HALF:
                        rope_sum(r, dve_q, job_count(c, k) - 1)
                    else:
                        rope_sum(r, s_rot, 1)
                    if i == 1:
                        rope_sum(r + 1, dve_q, job_count(c, k))
                if next_weights_at(c, k):
                    g = k + (c // 8) + 1
                    low(act_wq, g * 4 + (i + 1), lambda a: wq[:, a, i], raw_q[:, i % 2], s_wq)
                    if i == 1:
                        low(act_wk, g + 1, lambda a: wk[:, a], raw_k[:], s_wk)
                    if i == 3:
                        low(act_wv, g + 1, lambda a: wv[:, a], raw_v[:], s_wv)
                if next_output_at(c, k):
                    g = k + (c // 8) + 1
                    low(act_wo, g * 4 + (i + 1), wo_part(g, i), raw_o[:, i % 2], s_wo)
                fill(streams, pool, 4)

            schedule(pool, emit, "pool")

        @block.tensor
        def _(pe):
            def pairs(t, *head):
                return [[t[(slice(None), a) + head + (kc,)] for a in (0, 1)] for kc in range(K_CH)]

            def bank_read(c, k, job):
                i = c % HALF
                if (job, i) == ("q", 1):
                    if unit(c, k) > 0:
                        pe.wait_ge(dve_kv, kv_before(c, k))
                elif rope:
                    before = {("q", 0): 0, ("k", 1): 0, ("q", 2): -1, ("q", 3): -1, ("v", 3): 0}[job, i]
                    if unit(c, k) > -HALF:
                        pe.wait_ge(s_rot, rots_before(c, k) + before)
                elif (job, i) == ("q", 3):
                    pe.wait_ge(dve_kv, kv_before(c, k))
                elif unit(c, k) > -HALF:
                    pe.wait_ge(dve_q, job_count(c, k) - 1)

            def emit(c, k):
                i, half, nhalf = c % HALF, (c // HALF) % 2, (c // HALF + 1) % 2
                tok = slice(HALF * P * nhalf, HALF * P * (nhalf + 1))
                if valid(c, k, 0):
                    if i == 0:
                        pe.wait_ge(dve_q, job_count(c, k) - 1)
                        pe.wait_ge(dve_kv, kv_before(c, k) - 1)
                    if unit(c, k) >= 2:
                        pe.wait_ge(act_e, count(c, k, 2))
                    for h in range(n_heads):
                        m = product(pe, ps_s[:, c % 2, h], [[qT[:, half, a, h, i] for a in (0, 1)]],
                                    [[kT[:, half, a, i] for a in (0, 1)]])
                    m.then_inc(pe_s, 1)
                if valid(c, k, 1):
                    pe.wait_ge(dve_n, count(c, k, 1))
                    for h in range(n_heads):
                        m = pe.transpose(ps_t[:, h], prob[:, (c - 1) % 2, h], ident[:])
                    m.then_inc(pe_t, 1)
                if jobs_at(c, k):
                    g = k + (c + HALF) // N_BATCH
                    pe.wait_ge(s_wq, g * 4 + (i + 1))
                    bank_read(c, k, "q")
                    product(pe, ps_job[:, BANK_Q[i]], pairs(wq, i), [[xnT[:, a, kc, tok] for a in (0, 1)] for kc in range(K_CH)]).then_inc(pe_q, 1)
                    if i == 1:
                        if unit(c, k) < 0:
                            pe.wait_ge(s_ctx_split, K_CH)
                        pe.wait_ge(s_wk, g + 1)
                        bank_read(c, k, "k")
                        product(pe, ps_job[:, BANK_K], pairs(wk), [[ctxT[:, a, kc, tok] for a in (0, 1)] for kc in range(K_CH)]).then_inc(pe_kv, 1)
                    if i == 3:
                        pe.wait_ge(s_wv, g + 1)
                        bank_read(c, k, "v")
                        product(pe, ps_job[:, BANK_V], pairs(wv), [[ctxT[:, a, kc, tok] for a in (0, 1)] for kc in range(K_CH)]).then_inc(pe_kv, 1)
                if valid(c, k, 2):
                    g = k + (c - 2) // 8
                    pe.wait_ge(dve_o, count(c, k, 2))
                    pe.wait_ge(s_wo, g * 4 + 4)
                    if unit(c, k) >= 4:
                        pe.wait_ge(dve_x, count(c, k, 4))
                    if isinstance(g, int):
                        w_out = [[wo[:, g % 2, a, h] for a in (0, 1)] for h in range(n_heads)]
                    else:
                        w_out = [[wo[:, bass.ds(g % 2, 1), a, h].rearrange("p a n -> p (a n)") for a in (0, 1)] for h in range(n_heads)]
                    m = product(pe, ps_o[:, c % 2], [[oT[:, a, h] for a in (0, 1)] for h in range(n_heads)], w_out)
                    m.then_inc(pe_o, 1)
                if valid(c, k, 1):
                    pe.wait_ge(dve_t, count(c, k, 1))
                    b, hv = (c - 1) % HALF, ((c - 1) // HALF) % 2
                    if i == 1:
                        pe.wait_ge(dve_kv, kv_before(c, k))
                    m = product(pe, ps_v[:], [[vv[:, hv, a, b] for a in (0, 1)]], [[probT[:, a] for a in (0, 1)]])
                    m.then_inc(pe_pv, 1)
                if jobs_at(c, k) and i == 3:
                    pe.wait_ge(act_vt, halves(c, k))
                    for b in range(HALF):
                        m = pe.transpose(ps_job[:, BANK_V, b * P:(b + 1) * P], v_cols[:, b], ident[:])
                    m.then_inc(pe_vt, 1)

            pe.wait_ge(s_const, 16 * n_const)
            schedule(pe, emit)

        def column(t, base, per, k):
            return t[:, per * k + base:per * k + base + 1] if isinstance(k, int) else t[:, bass.ds(k * per + base, 1)]

        def job_bias(c, k, kind):
            g0 = (c + HALF) // N_BATCH
            if not biased:
                return None
            return column(bq, n_heads * g0 + c % HALF, n_heads, k) if kind == "q" else column(bk, g0, 1, k)

        def v_bias(c, k):
            return column(bv, (c - 1) // N_BATCH, 1, k) if biased else None

        @block.scalar
        def _(act):
            def act_wait_bias(s, value):
                act.wait_ge(s, value)
                if biased and not isinstance(value, int):
                    act.sem_inc(s_apart, 1)

            def high(dst, src, bias=None):
                if bias is None:
                    return act.copy(dst, src)
                return act.activation(dst, src, ACT.Identity, bias=bias)

            def emit(c, k):
                i, nhalf = c % HALF, (c // HALF + 1) % 2
                if valid(c, k, 1):
                    act.wait_ge(pe_t, count(c, k, 1))
                    high(probT[:, 0], ps_t[:]).then_inc(act_t, 1)
                if valid(c, k, 0):
                    act.wait_ge(dve_m, count(c, k))
                    for h in range(n_heads):
                        src = prob[:, c % 2, h] if rope else ps_s[:, c % 2, h]
                        m = act.activation(prob[:, c % 2, h], src, ACT.Exp, bias=negmax[:, c % 2, h:h + 1], scale=scale,
                                           accum_out=sums[:, c % 2, h:h + 1])
                    m.then_inc(act_e, 1)
                if jobs_at(c, k):
                    if rope:
                        act.wait_ge(s_sum, rots_before(c, k) + 1)
                        high(qT[:, nhalf, 0, i], roped[:]).then_inc(act_q, 1)
                    else:
                        act_wait_bias(pe_q, job_count(c, k))
                        high(qT[:, nhalf, 0, i], ps_job[:, BANK_Q[i]].rearrange("p (b t) -> p b t", b=HALF), job_bias(c, k, "q")).then_inc(act_q, 1)
                    if i == 1:
                        if rope:
                            act.wait_ge(s_sum, rots_before(c, k) + 2)
                            high(kT[:, nhalf, 0], roped[:]).then_inc(act_kv, 1)
                        else:
                            act_wait_bias(pe_kv, kv_before(c, k) + 1)
                            high(kT[:, nhalf, 0], ps_job[:, 0].rearrange("p (b t) -> p b t", b=HALF), job_bias(c, k, "k")).then_inc(act_kv, 1)
                    if i == 3:
                        act.wait_ge(pe_kv, kv_before(c, k) + 1)
                        act.copy(v_cols[:], ps_job[:, BANK_V].rearrange("p (b t) -> p b t", b=HALF)).then_inc(act_vt, 1)
                if valid(c, k, 1):
                    act_wait_bias(pe_pv, count(c, k, 1))
                    high(oT[:, 0], ps_v[:], v_bias(c, k)).then_inc(act_o, 1)
                if jobs_at(c, k) and i == 3:
                    act.wait_ge(pe_vt, halves(c, k))
                    high(vv[:, nhalf, 0], ps_job[:, BANK_V].rearrange("p (b t) -> p b t", b=HALF)).then_inc(act_kv, 1)
                next_weights(c, k)

            def weights(raw_sem, value, dst, raw, done):
                act.wait_ge(raw_sem, value)
                if not isinstance(value, int):
                    act.sem_inc(s_apart, 1)
                act.copy(dst, raw).then_inc(done, 1)

            def q_weights(g, j):
                weights(s_rawq[j % 2], g * 32 + 16 * (j // 2 + 1), wq[:, 0, j], raw_q[:, j % 2], act_wq)

            def k_weights(g):
                weights(s_rawk, g * 16 + 16, wk[:, 0], raw_k[:], act_wk)

            def v_weights(g):
                weights(s_rawv, g * 16 + 16, wv[:, 0], raw_v[:], act_wv)

            def next_weights(c, k):
                i, g = c % HALF, k + (c // 8) + 1
                if next_weights_at(c, k):
                    act.wait_ge(pe_q, job_count(c, k))
                    q_weights(g, i)
                    if i in (1, 3):
                        act.wait_ge(pe_kv, kv_before(c, k) + 1)
                        (k_weights if i == 1 else v_weights)(g)
                if next_output_at(c, k):
                    if unit(c, k) >= HALF and i == 0:
                        act.wait_ge(pe_o, count(c, k, 4))
                    weights(s_rawo[i % 2], g * 32 + 16 * (i // 2 + 1), wo_part(g, i)(0), raw_o[:, i % 2], act_wo)

            def ctx_high(kc):
                act.wait_ge(s_ctx[kc % 2], 16 * (kc // 2 + 1))
                act.copy(ctxT[:, 0, kc], ctx_raw[kc % 2]).then_inc(s_ctx_high, 1)

            q_weights(0, 0)
            ctx_high(0)
            q_weights(0, 1)
            k_weights(0)
            for kc in (1, 2, 3):
                ctx_high(kc)
            q_weights(0, 2)
            q_weights(0, 3)
            v_weights(0)
            act.wait_ge(s_const, 16 * n_const)
            schedule(act, emit)

        @block.vector
        def _(dve):
            def low(dst, src, high, bias=None):
                if bias is None:
                    return dve.tensor_tensor(dst, src, high, ALU.subtract)
                return dve.scalar_tensor_tensor(dst, src, bias, high, ALU.add, ALU.subtract)

            def rotate(bank, n_done):
                src = ps_job[:, bank].rearrange("p (b t) -> p b t", b=HALF)
                both = lambda t, lo, hi: t[lo:hi].unsqueeze(1).broadcast_to([hi - lo, HALF, P])
                if not (isinstance(n_done, int) and n_done == 0):
                    dve.wait_ge(s_sum, n_done)
                dve.tensor_tensor(rot_a[:], src, both(cosT, 0, P), ALU.mult)
                dve.tensor_tensor(rot_b[64:128], src[0:64], both(sinT, 0, 64), ALU.mult)
                dve.tensor_tensor(rot_b[0:64], src[64:128], both(sinT, 64, P), ALU.mult).then_inc(s_rot, 1)

            def emit(c, k):
                i, nhalf = c % HALF, (c // HALF + 1) % 2
                rots = rots_before(c, k)
                if valid(c, k, 0):
                    dve.wait_ge(pe_s, count(c, k))
                    if rope:
                        if unit(c, k) >= 2:
                            dve.wait_ge(pe_t, count(c, k, 2))
                        dve.tensor_tensor(prob[:, c % 2], ps_s[:, c % 2], mask[:].unsqueeze(1).broadcast_to([P, n_heads, P]), ALU.add)
                        dve.drain()
                        dve.tensor_reduce(negmax[:, c % 2], prob[:, c % 2], AX.X, ALU.max, negate=True)
                    else:
                        dve.tensor_reduce(negmax[:, c % 2], ps_s[:, c % 2], AX.X, ALU.max, negate=True)
                    dve.drain()
                    dve.tensor_scalar(negmax[:, c % 2], negmax[:, c % 2], scale, None, ALU.mult).then_inc(dve_m, 1)
                if valid(c, k, 1):
                    dve.wait_ge(act_t, count(c, k, 1))
                    low(probT[:, 1], ps_t[:], probT[:, 0]).then_inc(dve_t, 1)
                fill(streams, dve, TILE_STEPS)
                if jobs_at(c, k) and rope:
                    dve.wait_ge(pe_q, job_count(c, k))
                    rotate(BANK_Q[i], rots)
                if valid(c, k, 0):
                    dve.wait_ge(act_e, count(c, k))
                    dve.reciprocal(recip[:, c % 2], sums[:, c % 2])
                    dve.drain()
                    dve.tensor_tensor(prob[:, c % 2], prob[:, c % 2], recip[:, c % 2].unsqueeze(2).broadcast_to([P, n_heads, P]),
                                      ALU.mult).then_inc(dve_n, 1)
                fill(streams, dve, TILE_STEPS)
                if jobs_at(c, k):
                    dve.wait_ge(act_q, job_count(c, k))
                    if rope:
                        low(qT[:, nhalf, 1, i], roped[:], qT[:, nhalf, 0, i]).then_inc(dve_q, 1)
                    else:
                        low(qT[:, nhalf, 1, i], ps_job[:, BANK_Q[i]].rearrange("p (b t) -> p b t", b=HALF), qT[:, nhalf, 0, i],
                            job_bias(c, k, "q")).then_inc(dve_q, 1)
                    if i == 1:
                        if rope:
                            dve.wait_ge(pe_kv, kv_before(c, k) + 1)
                            rotate(0, rots + 1)
                            dve.wait_ge(act_kv, kv_before(c, k) + 1)
                            low(kT[:, nhalf, 1], roped[:], kT[:, nhalf, 0]).then_inc(dve_kv, 1)
                        else:
                            dve.wait_ge(act_kv, kv_before(c, k) + 1)
                            low(kT[:, nhalf, 1], ps_job[:, 0].rearrange("p (b t) -> p b t", b=HALF), kT[:, nhalf, 0], job_bias(c, k, "k")).then_inc(dve_kv, 1)
                fill(streams, dve, TILE_STEPS)
                if biased and unit(c, k) == 2:
                    dve.wait_ge(s_xb, 1)
                if valid(c, k, 2):
                    dve.wait_ge(pe_o, count(c, k, 2))
                    x_b = resid[:, (c - 2) % 8]
                    dve.tensor_tensor(x_b, ps_o[:, c % 2], x_b, ALU.add).then_inc(dve_x, 1)
                fill(streams, dve, TILE_STEPS)
                if valid(c, k, 1):
                    dve.wait_ge(act_o, count(c, k, 1))
                    low(oT[:, 1], ps_v[:], oT[:, 0], v_bias(c, k)).then_inc(dve_o, 1)
                if jobs_at(c, k) and i == 3:
                    dve.wait_ge(act_kv, kv_before(c, k) + 1)
                    low(vv[:, nhalf, 1], ps_job[:, BANK_V].rearrange("p (b t) -> p b t", b=HALF), vv[:, nhalf, 0]).then_inc(dve_kv, 1)

            def q_low(j):
                dve.wait_ge(act_wq, j + 1)
                low(wq[:, 1, j], raw_q[:, j % 2], wq[:, 0, j]).then_inc(s_wq, 1)

            def ctx_low(kc):
                dve.wait_ge(s_ctx_high, kc + 1)
                low(ctxT[:, 1, kc], ctx_raw[kc % 2], ctxT[:, 0, kc]).then_inc(s_ctx_split, 1)

            q_low(0)
            ctx_low(0)
            q_low(1)
            dve.wait_ge(act_wk, 1)
            low(wk[:, 1], raw_k[:], wk[:, 0]).then_inc(s_wk, 1)
            for kc in (1, 2, 3):
                ctx_low(kc)
            q_low(2)
            q_low(3)
            dve.wait_ge(act_wv, 1)
            low(wv[:, 1], raw_v[:], wv[:, 0]).then_inc(s_wv, 1)
            dve.wait_ge(s_const, 16 * n_const)
            schedule(dve, emit, "dve")


def expert_group_and_permuted_ffn(nc, resid, xnT, w, codes, tiles):
    E, R = 8, 16
    GATES = E + 1
    NL = E * R + GATES + 1
    H2 = 16
    with ExitStack() as stack:
        sb = lambda name, shape, dt=F32: stack.enter_context(nc.sbuf_tensor("c_" + name, shape, dt))
        sem = lambda name: stack.enter_context(nc.semaphore("c_" + name))
        wb = sb("wb", [P, 2, K_CH, D], F32R)
        wl = sb("wl", [P, 2, K_CH, NL], F32R)
        wB = sb("wB", [P, 2, D], F32R)
        up = sb("up", [P, 2, 4, P], F32R)
        down = sb("down", [P, 2, H2, P], F32R)
        wp, wg, wm = sb("wp", [P, 2, P], F32R), sb("wg", [P, 2, P], F32R), sb("wm", [P, 2, P], F32R)
        pick, pickT = sb("pick", [P, K_CH, D], F32R), sb("pickT", [P, K_CH, D], F32R)
        group_ones, ident = sb("group_ones", [P, P]), sb("ident", [P, P])
        gn_w, gn_b, thr_b = sb("gn_w", [P, 1]), sb("gn_b", [P, 1]), sb("thr_b", [P, 1])
        bias_b = sb("bias_b", [P, D])
        ps = stack.enter_context(nc.psum_tensor("c_ps", [P, 8, 512], F32))

        s_raw, s_high = [sem("raw0"), sem("raw1")], sem("high")
        s_const, s_setup, s_pick, s_set2, s_zero, s_ctx, apart = (sem(n) for n in ("const", "setup", "pick", "product", "zero", "ctx", "apart"))
        pe_s = Steps(sem("pe"), both("xT") + both("low") + both("base") + both("hT") + both("ffn") + [(n, j) for j in (0, 1) for n in ("g", "p", "y")]
                     + [("grp", 0)] + both("xT2") + both("perm")
                     + [(n, j) for j in (0, 1) for n in ("up0", "up1", "up2", "up3", "down", "out")] + both("xnT"))
        act_s = Steps(sem("act"), both("xT") + both("gates") + both("thr") + both("hT") + both("cs") + both("xs") + both("g")
                      + both("yn") + both("xT2") + both("xp") + [(n, j) for j in (0, 1) for n in ("up0", "up1", "up2", "up3", "yT")] + both("xnT"))
        dve_s = Steps(sem("dve"), both("xn") + both("xT") + [("gneg", 0)] + both("hw") + both("hT") + both("x1") + both("xn2")
                      + both("p") + [("row", 0), ("affine", 0)] + both("x2") + both("xn3") + both("xT2") + both("xp")
                      + [(n, j) for j in (0, 1) for n in ("up0", "up1", "up2", "up3", "yT")] + both("x3") + both("xn4") + both("resid") + both("xnT"))
        pool_s = Steps(sem("pool"), both("cs") + both("xs") + both("x1c") + [(n, j) for j in (0, 1) for n in ("up0", "up1", "up2", "up3")])
        steps = {"pe": pe_s, "act": act_s, "dve": dve_s, "pool": pool_s}

        def wait_for(eng, k, *names, apart_for=False):
            for who, name, j in names:
                eng.wait_ge(steps[who].sem, steps[who].value((name, j), k))
            if apart_for and not isinstance(k, int):
                eng.sem_inc(apart, 1)

        waits = wait_for

        def waits_before(eng, k, *names, apart_for=False):
            for who, name, j in names:
                s = steps[who]
                v = s.value((name, j), k) - len(s.names)
                if isinstance(v, int) and v <= 0:
                    continue
                eng.wait_ge(s.sem, v)
            if apart_for and not isinstance(k, int):
                eng.sem_inc(apart, 1)

        with ExitStack() as once:
            tmp = lambda name, shape, dt=F32: once.enter_context(nc.sbuf_tensor("c_" + name, shape, dt))
            raw = tmp("raw", [P, 2, 2048])
            wt_raw, wz_raw = tmp("wt_raw", [P, P]), tmp("wz_raw", [P, P])
            iota_row, iota_col = tmp("iota_row", [P, D]), tmp("iota_col", [P, K_CH])
            perm_row_i, perm_col_i = tmp("perm_row_i", [P, D], I32), tmp("perm_col_i", [P, K_CH], I32)
            perm_row, perm_col = tmp("perm_row", [P, D]), tmp("perm_col", [P, K_CH])
            setup = once.enter_context(nc.Block())

            staged = [(wb, w["wb"], K_CH * D), (wl, w["wl"], K_CH * NL), (wB, w["wB"], D), (up, w["up"], 4 * P),
                      (down, w["down"], H2 * P), (wp, w["wp"], P), (wg, w["wg"], P)]
            consts = [(wt_raw, w["wt"]), (iota_row, w["iota"].broadcast_to([P, D])), (iota_col, w["iota_col"]), (perm_row_i, w["perm"].broadcast_to([P, D])),
                      (perm_col_i, w["perm_col"]), (group_ones, w["group_ones"]), (ident, w["ident"]), (gn_w, w["gn_w"]), (gn_b, w["gn_b"]),
                      (thr_b, w["thr_b"].broadcast_to([P, 1])), (bias_b, w["bias_b"].broadcast_to([P, D]))]
            n_const = len(consts) + 8

            @setup.sync
            def _(sp):
                for n, (dst, src, cols) in enumerate(staged):
                    if n == 2:
                        for const, const_src in consts:
                            sp.dma_start(const[:], const_src).then_inc(s_const, 16)
                        sp.wait_ge(s_zero, 1)
                        for g in range(8):
                            sp.dma_start(wz_raw[16 * g:16 * g + 16, 16 * g:16 * g + 16], w["wz"][g]).then_inc(s_const, 16)
                    if n >= 2:
                        sp.wait_ge(s_setup, n - 1)
                    if dst is down:
                        sp.wait_ge(s_zero, 2)
                        for r in range(4):
                            sp.dma_start(raw[:, n % 2].rearrange("p (c r m) -> p c r m", c=4, r=4)[:, :, r, 32 * r:32 * r + 32],
                                         src[:, :, r]).then_inc(s_raw[n % 2], 16)
                    else:
                        sp.dma_start(raw[:, n % 2, 0:cols], src).then_inc(s_raw[n % 2], 16)

            views = []
            for n, (dst, src, cols) in enumerate(staged):
                flat = dst[:] if len(dst.shape) == 3 else dst[:].rearrange("p a k n -> p a (k n)")
                views.append((flat[:, 0], flat[:, 1], raw[:, n % 2, 0:cols]))

            @setup.gpsimd
            def _(pool):
                pool.memset(wz_raw[:], 0.0).then_inc(s_zero, 1)
                n = [dst for dst, _, _ in staged].index(down)
                pool.wait_ge(s_setup, n - 1)
                pool.memset(raw[:, n % 2], 0.0).then_inc(s_zero, 1)

            @setup.tensor
            def _(pe):
                pe.wait_ge(s_const, 16 * n_const)
                pe.matmul(ps[:, 0, 0:P], wt_raw[:], wz_raw[:], start=True, stop=True).then_inc(s_set2, 1)
                pe.wait_ge(s_set2, 3)
                pe.wait_ge(s_pick, 1)
                pe.wait_ge(s_setup, len(staged))

            @setup.scalar
            def _(act):
                got = [0, 0]
                for n, (hi, lo, src) in enumerate(views):
                    got[n % 2] += 4 if staged[n][0] is down else 1
                    act.wait_ge(s_raw[n % 2], 16 * got[n % 2])
                    act.copy(hi, src).then_inc(s_high, 1)
                act.wait_ge(s_set2, 1)
                act.copy(wm[:, 0], ps[:, 0, 0:P]).then_inc(s_set2, 1)

            def tables(dve):
                dve.wait_ge(s_const, 16 * n_const)
                dve.tensor_scalar(thr_b[:], thr_b[:], -1.0, None, ALU.mult)
                dve.tensor_copy(perm_row[:], perm_row_i[:])
                dve.tensor_copy(perm_col[:], perm_col_i[:])
                dve.drain()
                for c in range(K_CH):
                    dve.tensor_scalar(pick[:, c], perm_row[:], iota_col[:, c:c + 1], None, ALU.is_equal)
                    i = dve.tensor_scalar(pickT[:, c], iota_row[:], perm_col[:, c:c + 1], None, ALU.is_equal)
                i.then_inc(s_pick, 1)

            @setup.vector
            def _(dve):
                for n, (hi, lo, src) in enumerate(views):
                    if n == 2:
                        tables(dve)
                    dve.wait_ge(s_high, n + 1)
                    dve.tensor_tensor(lo, src, hi, ALU.subtract).then_inc(s_setup, 1)
                dve.wait_ge(s_set2, 2)
                dve.tensor_tensor(wm[:, 1], ps[:, 0, 0:P], wm[:, 0], ALU.subtract).then_inc(s_set2, 1)

        ctx_in = sb("ctx_in", [P, 2, D])
        cs = sb("cs", [P, 2, 2, D], F32R)
        x = sb("x", [P, 2, D])
        xn = sb("xn", [P, 2, D])
        xs = sb("xs", [P, 2, 2, D], F32R)
        xT = sb("xT", [P, 2, 2, K_CH, P], F32R)
        gate, gsum, thr, wgate, wsum, wzero = (sb(n, [P, 2, m]) for n, m in
                                               (("gate", E), ("gsum", 1), ("thr", 1), ("wgate", E), ("wsum", 1), ("wzero", 1)))
        gneg = sb("gneg", [P, 2, 1])
        hw = sb("hw", [P, 2, P])
        hT = sb("hT", [P, 2, 2, P], F32R)
        g_sb, gp = sb("g_sb", [P, 2, D]), sb("gp", [P, D])
        row = sb("row", [P, 2, 3])
        ystats, ymv = sb("ystats", [P, 2, 6]), sb("ymv", [P, 2, 2])
        grp, gvar, grstd, gtmp = sb("grp", [P, 2, 3]), sb("gvar", [P, 2]), sb("grstd", [P, 2]), sb("gtmp", [P, 2])
        g_a, g_b = sb("g_a", [P, 2]), sb("g_b", [P, 2])
        yn = sb("yn", [P, 2, D])
        xp = sb("xp", [P, 2, 2, 4, P], F32R)
        act_f = sb("act_f", [P, 2, 4, P])
        acts = sb("acts", [P, 2, H2, P], F32R)
        yT = sb("yT", [P, 2, 2, 4, P], F32R)
        norm = Norm(sb, "norm")

        PAIRS = N_BATCH // 2
        streams = {who: CodeTiles(nc, stack, "c_n_" + who, codes, apart, who, *tile, PAIRS) for who, tile in tiles.items()}
        block = stack.enter_context(nc.Block())

        def loop(eng, emit):
            emit(0)
            with eng.Fori(1, PAIRS) as k:
                emit(k)

        @block.sync
        def _(sp):
            def emit(k):
                waits_before(sp, k, ("act", "cs", 1), ("pool", "x1c", 1))
                sp.dma_start(ctx_in[:], w["ctx"][bass.ds(2 * k, 2)].rearrange("b p d -> p b d")).then_inc(s_ctx, 16)
                turn(streams, sp, k)
            for st in streams.values():
                st.start(sp)
            loop(sp, emit)
            for st in streams.values():
                st.finish(sp)

        @block.gpsimd
        def _(pool):
            def emit(k):
                begin(streams, pool, "pool", k)
                fill(streams, pool, 8)
                for j in (0, 1):
                    waits(pool, k, ("act", "cs", j))
                    pool_s.done(pool.tensor_tensor(cs[:, 1, j], ctx_in[:, j], cs[:, 0, j], ALU.subtract), ("cs", j))
                for j in (0, 1):
                    waits(pool, k, ("act", "xs", j))
                    pool_s.done(pool.tensor_tensor(xs[:, 1, j], xn[:, j], xs[:, 0, j], ALU.subtract), ("xs", j))
                for j in (0, 1):
                    waits(pool, k, ("dve", "xn2", j))
                    pool_s.done(pool.tensor_tensor(x[:, j], x[:, j], ctx_in[:, j], ALU.add), ("x1c", j))
                fill(streams, pool)
                for j in (0, 1):
                    for r in range(4):
                        waits(pool, k, ("dve", f"up{r}", j))
                        pool_s.done(pool.tensor_tensor(acts[:, 1, 4 * r:4 * r + 4], act_f[:, r % 2], acts[:, 0, 4 * r:4 * r + 4], ALU.subtract), (f"up{r}", j))
            loop(pool, emit)

        @block.tensor
        def _(pe):
            def emit(k):
                chunk = lambda c: slice(c * P, (c + 1) * P)

                def turn(step, bank, src, before=()):
                    for j in (0, 1):
                        waits(pe, k, ("dve", step[1], j))
                        waits_before(pe, k, *before)
                        for c in range(4):
                            i = pe.transpose(ps[:, bank + j, chunk(c)], src[:, j, chunk(c)], ident[:])
                        pe_s.done(i, (step[0], j))

                turn(("xT", "xn"), 0, xn)
                for j in (0, 1):
                    waits(pe, k, ("dve", "xT", j))
                    pe_s.done(product(pe, ps[:, 2 + j, 0:NL], [hi_lo(xT, j, c) for c in range(K_CH)], [hi_lo(wl, c) for c in range(K_CH)]), ("low", j))
                for j in (0, 1):
                    pe_s.done(product(pe, ps[:, 4 + j], [hi_lo(xT, j, c) for c in range(K_CH)], [hi_lo(wb, c) for c in range(K_CH)], last=False), ("base", j))
                for j in (0, 1):
                    waits(pe, k, ("dve", "hw", j))
                    pe_s.done(pe.transpose(ps[:, j, 0:P], hw[:, j], ident[:]), ("hT", j))
                for j in (0, 1):
                    waits(pe, k, ("dve", "hT", j))
                    pe_s.done(product(pe, ps[:, 4 + j], [hi_lo(hT, j)], [hi_lo(wB)], first=False), ("ffn", j))
                for j in (0, 1):
                    waits(pe, k, ("pool", "cs", j))
                    if j == 1:
                        waits(pe, k, ("act", "g", 0))
                    pe_s.done(product(pe, ps[:, 0], [hi_lo(wg)], [hi_lo(cs, j)]), ("g", j))
                    waits(pe, k, ("pool", "xs", j))
                    if j == 1:
                        waits(pe, k, ("dve", "p", 0))
                    pe_s.done(product(pe, ps[:, 1], [hi_lo(wp)], [hi_lo(xs, j)]), ("p", j))
                    pe_s.done(product(pe, ps[:, 2 + j], [hi_lo(wm)], [hi_lo(cs, j)]), ("y", j))
                waits(pe, k, ("dve", "row", 0))
                pe_s.done(pe.matmul(ps[:, 4, 0:6], group_ones[:], row[:].rearrange("p b s -> p (b s)"), start=True, stop=True), ("grp", 0))
                turn(("xT2", "xn3"), 0, xn)
                for j in (0, 1):
                    waits(pe, k, ("dve", "xT2", j))
                    for c in range(4):
                        i = product(pe, ps[:, 2 + j, chunk(c)], [[pick[:, kc, chunk(c)]] for kc in range(K_CH)], [hi_lo(xT, j, kc) for kc in range(K_CH)])
                    pe_s.done(i, ("perm", j))
                for j in (0, 1):
                    waits(pe, k, ("dve", "xp", j))
                    for r in range(4):
                        if j == 1:
                            waits(pe, k, ("dve", f"up{r}", 0))
                        rows = slice(32 * r, 32 * r + 32)
                        for c in range(4):
                            i = product(pe, ps[:, 4 + r, chunk(c)], [[up[rows, a, c] for a in (0, 1)]], [[xp[rows, a, j, c] for a in (0, 1)]])
                        pe_s.done(i, (f"up{r}", j))
                    waits(pe, k, ("pool", "up3", j))
                    for c in range(4):
                        i = product(pe, ps[:, j, chunk(c)], [hi_lo(down, 4 * c + r) for r in range(4)], [hi_lo(acts, 4 * r + c) for r in range(4)])
                    pe_s.done(i, ("down", j))
                    waits(pe, k, ("dve", "yT", j))
                    pe_s.done(product(pe, ps[:, 2 + j], [hi_lo(yT, j, c) for c in range(4)], [[pickT[:, c]] for c in range(4)]), ("out", j))
                turn(("xnT", "xn4"), 0, xn)
            loop(pe, emit)

        @block.scalar
        def _(act):
            def emit(k):
                four = lambda t: t.rearrange("p (c t) -> p c t", c=4)
                for j in (0, 1):
                    waits(act, k, ("pe", "xT", j))
                    act_s.done(act.copy(xT[:, 0, j], four(ps[:, j])), ("xT", j))
                for j in (0, 1):
                    waits(act, k, ("dve", "gneg", 0))
                    act_s.done(act.activation(gate[:, j], ps[:, 2 + j, E * R:E * R + E], ACT.Exp, bias=gneg[:, j], accum_out=gsum[:, j]), ("gates", j))
                for j in (0, 1):
                    act_s.done(act.activation(thr[:, j], ps[:, 2 + j, E * R + E:E * R + E + 1], ACT.Exp, bias=thr_b[:], scale=-1.0), ("thr", j))
                for j in (0, 1):
                    waits(act, k, ("pe", "hT", j))
                    act_s.done(act.copy(hT[:, 0, j], ps[:, j, 0:P]), ("hT", j))
                act.wait_ge(s_ctx, k * 16 + 16)
                for j in (0, 1):
                    act_s.done(act.copy(cs[:, 0, j], ctx_in[:, j]), ("cs", j))
                for j in (0, 1):
                    waits(act, k, ("dve", "xn2", j))
                    act_s.done(act.copy(xs[:, 0, j], xn[:, j]), ("xs", j))
                for j in (0, 1):
                    waits(act, k, ("pe", "g", j))
                    act_s.done(act.copy(g_sb[:, j], ps[:, 0]), ("g", j))
                for j in (0, 1):
                    waits(act, k, ("dve", "affine", 0))
                    act_s.done(act.activation(yn[:, j], ps[:, 2 + j], ACT.Identity, bias=g_b[:, j:j + 1], scale=g_a[:, j:j + 1]), ("yn", j))
                for j in (0, 1):
                    waits(act, k, ("pe", "xT2", j))
                    act_s.done(act.copy(xT[:, 0, j], four(ps[:, j])), ("xT2", j))
                for j in (0, 1):
                    waits(act, k, ("pe", "perm", j))
                    act_s.done(act.copy(xp[:, 0, j], four(ps[:, 2 + j])), ("xp", j))
                for j in (0, 1):
                    for r in range(4):
                        waits(act, k, ("pe", f"up{r}", j))
                        if r >= 2:
                            waits(act, k, ("pool", f"up{r - 2}", j))
                        elif j == 1:
                            waits(act, k, ("pool", f"up{r + 2}", 0))
                        else:
                            waits_before(act, k, ("pool", f"up{r + 2}", 1))
                        act_s.done(act.activation(act_f[:, r % 2], four(ps[:, 4 + r]), ACT.Gelu), (f"up{r}", j))
                    waits(act, k, ("pe", "down", j))
                    act_s.done(act.copy(yT[:, 0, j], four(ps[:, j])), ("yT", j))
                for j in (0, 1):
                    waits(act, k, ("pe", "xnT", j), apart_for=True)
                    act_s.done(act.copy(xnT[:, 0, :, bass.ds(2 * P * k + j * P, P)], four(ps[:, j])), ("xnT", j))
            loop(act, emit)

        @block.vector
        def _(dve):
            def waits(eng, k, *names, apart_for=False):
                fill(streams, dve, 2)
                wait_for(eng, k, *names, apart_for=apart_for)

            def emit(k):
                begin(streams, dve, "dve", k)
                four = lambda t: t.rearrange("p (c t) -> p c t", c=4)
                xn_of = [xn[:, j] for j in (0, 1)]

                def turned(step, dst, bank, **kw):
                    for j in (0, 1):
                        waits(dve, k, ("act", step, j), **kw)
                        dve_s.done(dve.tensor_tensor(dst(1, j), four(ps[:, bank + j]), dst(0, j), ALU.subtract), (step, j))

                dve.drain()
                for j in (0, 1):
                    i = dve.tensor_copy(x[:, j], resid[:, bass.ds(2 * k + j, 1)].rearrange("p a d -> p (a d)"))
                dve.drain()
                norm.emit(dve, [x[:, j] for j in (0, 1)], xn_of, lambda i, j: dve_s.done(i, ("xn", j)))
                turned("xT", lambda a, j: xT[:, a, j], 0)
                waits(dve, k, ("pe", "low", 1))
                for j in (0, 1):
                    i = dve.tensor_reduce(gneg[:, j], ps[:, 2 + j, E * R:E * R + E], AX.X, ALU.max, negate=True)
                dve_s.done(i, ("gneg", 0))
                waits(dve, k, ("act", "thr", 1))
                dve.tensor_scalar(thr[:], thr[:], 1.0, None, ALU.add)
                dve.reciprocal(gsum[:], gsum[:])
                dve.drain()
                dve.reciprocal(thr[:], thr[:])
                dve.tensor_tensor(gate[:], gate[:], gsum[:].broadcast_to([P, 2, E]), ALU.mult)
                dve.drain()
                dve.tensor_scalar(thr[:], thr[:], 0.125, None, ALU.mult)
                dve.drain()
                dve.tensor_tensor(wgate[:], gate[:], thr[:].broadcast_to([P, 2, E]), ALU.subtract)
                dve.drain()
                dve.tensor_scalar(wgate[:], wgate[:], 0.0, None, ALU.max)
                dve.drain()
                dve.tensor_reduce(wsum[:], wgate[:], AX.X, ALU.add)
                dve.drain()
                dve.tensor_scalar(wzero[:], wsum[:], 0.0, None, ALU.is_equal)
                dve.drain()
                dve.tensor_tensor(wsum[:], wsum[:], wzero[:], ALU.add)
                dve.drain()
                dve.reciprocal(wsum[:], wsum[:])
                dve.drain()
                dve.tensor_tensor(wgate[:], wgate[:], wsum[:].broadcast_to([P, 2, E]), ALU.mult)
                dve.drain()
                dve.tensor_scalar(wgate[:], wgate[:], 2.0, None, ALU.mult)
                dve.drain()
                for j in (0, 1):
                    dve_s.done(dve.tensor_tensor(hw[:, j].rearrange("p (e r) -> p e r", e=E), ps[:, 2 + j, 0:E * R].rearrange("p (e r) -> p e r", e=E),
                                                 wgate[:, j].unsqueeze(2).broadcast_to([P, E, R]), ALU.mult), ("hw", j))
                for j in (0, 1):
                    waits(dve, k, ("act", "hT", j))
                    dve_s.done(dve.tensor_tensor(hT[:, 1, j], ps[:, j, 0:P], hT[:, 0, j], ALU.subtract), ("hT", j))
                for j in (0, 1):
                    dve.tensor_tensor(x[:, j], x[:, j], bias_b[:], ALU.add)
                dve.drain()
                for j in (0, 1):
                    waits(dve, k, ("pe", "ffn", j))
                    dve_s.done(dve.tensor_tensor(x[:, j], ps[:, 4 + j], x[:, j], ALU.add), ("x1", j))
                dve.drain()
                norm.emit(dve, [x[:, j] for j in (0, 1)], xn_of, lambda i, j: dve_s.done(i, ("xn2", j)))
                for j in (0, 1):
                    waits(dve, k, ("pe", "p", j), ("act", "g", j), apart_for=True)
                    dve_s.done(dve.tensor_tensor_reduce(gp[:], ps[:, 1], g_sb[:, j], 1.0, 0.0, ALU.mult, ALU.add, row[:, j, 0:1]), ("p", j))
                waits(dve, k, ("pe", "y", 1))
                for j in (0, 1):
                    dve.bn_stats(ystats[:, j], ps[:, 2 + j])
                dve.drain()
                for j in (0, 1):
                    dve.bn_aggr(ymv[:, j], ystats[:, j])
                dve.drain()
                dve.tensor_copy(row[:, :, 1], ymv[:, :, 0])
                dve.tensor_tensor(row[:, :, 2], ymv[:, :, 0], ymv[:, :, 0], ALU.mult)
                dve.drain()
                dve_s.done(dve.tensor_tensor(row[:, :, 2], row[:, :, 2], ymv[:, :, 1], ALU.add), ("row", 0))
                waits(dve, k, ("pe", "grp", 0))
                dve.tensor_copy(grp[:].rearrange("p b s -> p (b s)"), ps[:, 4, 0:6])
                dve.drain()
                dve.tensor_scalar(grp[:, :, 1:3], grp[:, :, 1:3], 1.0 / 16.0, None, ALU.mult)
                dve.drain()
                dve.tensor_tensor(gtmp[:], grp[:, :, 1], grp[:, :, 1], ALU.mult)
                dve.drain()
                dve.tensor_tensor(gvar[:], grp[:, :, 2], gtmp[:], ALU.subtract)
                dve.tensor_tensor(grstd[:], grp[:, :, 0], grp[:, :, 0], ALU.mult)
                dve.drain()
                dve.tensor_tensor(gvar[:], gvar[:], grstd[:], ALU.mult)
                dve.drain()
                dve.tensor_scalar(gvar[:], gvar[:], EPS, None, ALU.add)
                dve.drain()
                inverse_root(dve, grstd[:], gvar[:], gtmp[:])
                dve.tensor_tensor(g_a[:], grp[:, :, 0], grstd[:], ALU.mult)
                dve.drain()
                dve.tensor_scalar(g_a[:], g_a[:], gn_w[:], None, ALU.mult)
                dve.drain()
                dve.tensor_tensor(g_b[:], grp[:, :, 1], g_a[:], ALU.mult)
                dve.drain()
                dve_s.done(dve.tensor_scalar(g_b[:], g_b[:], -1.0, gn_b[:], ALU.mult, ALU.add), ("affine", 0))
                for j in (0, 1):
                    waits(dve, k, ("act", "yn", j), ("pool", "x1c", j))
                    dve_s.done(dve.tensor_tensor(x[:, j], yn[:, j], x[:, j], ALU.add), ("x2", j))
                dve.drain()
                norm.emit(dve, [x[:, j] for j in (0, 1)], xn_of, lambda i, j: dve_s.done(i, ("xn3", j)))
                turned("xT2", lambda a, j: xT[:, a, j], 0)
                turned("xp", lambda a, j: xp[:, a, j], 2)
                for j in (0, 1):
                    for r in range(4):
                        waits(dve, k, ("act", f"up{r}", j))
                        dve_s.done(dve.tensor_copy(acts[:, 0, 4 * r:4 * r + 4], act_f[:, r % 2]), (f"up{r}", j))
                    waits(dve, k, ("act", "yT", j))
                    dve_s.done(dve.tensor_tensor(yT[:, 1, j], four(ps[:, j]), yT[:, 0, j], ALU.subtract), ("yT", j))
                for j in (0, 1):
                    waits(dve, k, ("pe", "out", j))
                    dve_s.done(dve.tensor_tensor(x[:, j], ps[:, 2 + j], x[:, j], ALU.add), ("x3", j))
                dve.drain()
                norm.emit(dve, [x[:, j] for j in (0, 1)], xn_of, lambda i, j: dve_s.done(i, ("xn4", j)))
                for j in (0, 1):
                    dve_s.done(dve.tensor_copy(resid[:, bass.ds(2 * k + j, 1)].rearrange("p a d -> p (a d)"), x[:, j]), ("resid", j))
                turned("xnT", lambda a, j: xnT[:, a, :, bass.ds(2 * P * k + j * P, P)], 0, apart_for=True)
                fill(streams, dve)
            loop(dve, emit)


def swiglu(nc, resid, xnT, scratch, ident_dram, out):
    w1d, w2d, w3d = scratch
    HID = w1d.shape[0]
    NH = (HID + P - 1) // P
    HALF = 4
    rows = [min(P, HID - P * c) for c in range(NH)]
    with ExitStack() as stack:
        sb = lambda name, shape, dt=F32: stack.enter_context(nc.sbuf_tensor("e_" + name, shape, dt))
        sem = lambda name: stack.enter_context(nc.semaphore("e_" + name))
        w1 = sb("w1", [P, 2, K_CH, HID], F32R)
        w2 = sb("w2", [P, 2, K_CH, HID], F32R)
        w3 = sb("w3", [P, 2, NH, D], F32R)
        ps = stack.enter_context(nc.psum_tensor("e_ps", [P, 8, 512], F32))
        ident = sb("ident", [P, P])
        s_in, s_id, s_t, s_hi, s_lo = [sem(f"in{i}") for i in range(4)], sem("id"), sem("t"), sem("hi"), sem("lo")
        s_xn, s_xt, s_xhi, s_xlo = (sem(n) for n in ("xn", "xt", "xhi", "xlo"))

        weights = [(m, c) for m in (0, 1, 2) for c in range(NH)]
        work = []
        for n in range(len(weights)):
            pair, at = n // 8, n % 8
            if at == 0 and pair < N_BATCH // 2:
                work.append(("norm", pair))
            work.append(("weight", n))
            if at in (4, 7) and pair < N_BATCH // 2:
                work.append(("turn", 2 * pair + (at == 7)))
        SLOTS, BANKS = 4, 4
        with ExitStack() as once:
            tmp = lambda name, shape: once.enter_context(nc.sbuf_tensor("e_" + name, shape, F32))
            nat, xn = tmp("nat", [P, SLOTS, D]), tmp("xn", [P, 4, D])
            norm = Norm(tmp, "norm")
            block = once.enter_context(nc.Block())

            def weight_views(n, part):
                m, c = weights[n]
                r = rows[c]
                if m < 2:
                    return (w1, w2)[m][:, part, :, c * P:c * P + r], ps[:, n % BANKS].rearrange("p (q h) -> p q h", q=4)[:, :, 0:r]
                return w3[0:r, part, c], ps[0:r, n % BANKS]

            def turn_views(b, part):
                return xnT[:, part, :, b * P:(b + 1) * P], ps[:, BANKS + b % 4].rearrange("p (c t) -> p c t", c=K_CH)

            @block.sync
            def _(sp):
                sp.dma_start(ident[:], ident_dram).then_inc(s_id, 16)
                for n, (m, c) in enumerate(weights):
                    if n >= SLOTS:
                        sp.wait_ge(s_t, n - SLOTS + 1)
                    r = rows[c]
                    if m < 2:
                        src = (w1d, w2d)[m][c * P:c * P + r, :]
                        sp.dma_start(nat[0:r, n % SLOTS], src).then_inc(s_in[n % SLOTS], 16)
                    else:
                        src = w3d.rearrange("(q p) h -> p q h", p=P)[:, :, c * P:c * P + r]
                        sp.dma_start(nat[:, n % SLOTS].rearrange("p (q h) -> p q h", q=4)[:, :, 0:r], src).then_inc(s_in[n % SLOTS], 16)

            @block.tensor
            def _(pe):
                pe.wait_ge(s_id, 16)
                for kind, n in work:
                    if kind == "weight":
                        m, c = weights[n]
                        r = rows[c]
                        pe.wait_ge(s_in[n % SLOTS], 16 * (n // SLOTS + 1))
                        if n >= BANKS:
                            pe.wait_ge(s_lo, n - BANKS + 1)
                        for q in range(4):
                            if m < 2:
                                i = pe.transpose(ps[:, n % BANKS, q * P:q * P + r], nat[0:r, n % SLOTS, q * P:(q + 1) * P], ident[0:r, 0:r])
                            else:
                                i = pe.transpose(ps[0:r, n % BANKS, q * P:(q + 1) * P], nat[:, n % SLOTS, q * P:q * P + r], ident[:])
                        i.then_inc(s_t, 1)
                    elif kind == "turn":
                        pe.wait_ge(s_xn, n + 1)
                        if n >= 4:
                            pe.wait_ge(s_xlo, n - 3)
                        for c in range(K_CH):
                            i = pe.transpose(ps[:, BANKS + n % 4, c * P:(c + 1) * P], xn[:, n % 4, c * P:(c + 1) * P], ident[:])
                        i.then_inc(s_xt, 1)

            @block.scalar
            def _(act):
                for kind, n in work:
                    if kind == "weight":
                        act.wait_ge(s_t, n + 1)
                        dst, src = weight_views(n, 0)
                        act.copy(dst, src).then_inc(s_hi, 1)
                    elif kind == "turn":
                        act.wait_ge(s_xt, n + 1)
                        dst, src = turn_views(n, 0)
                        act.copy(dst, src).then_inc(s_xhi, 1)

            @block.vector
            def _(dve):
                for kind, n in work:
                    if kind == "weight":
                        dve.wait_ge(s_hi, n + 1)
                        lo, src = weight_views(n, 1)
                        dve.tensor_tensor(lo, src, weight_views(n, 0)[0], ALU.subtract).then_inc(s_lo, 1)
                    elif kind == "turn":
                        dve.wait_ge(s_xhi, n + 1)
                        lo, src = turn_views(n, 1)
                        dve.tensor_tensor(lo, src, turn_views(n, 0)[0], ALU.subtract).then_inc(s_xlo, 1)
                    else:
                        if n >= 2:
                            dve.wait_ge(s_xt, 2 * n - 2)
                        norm.emit(dve, [resid[:, 2 * n + j] for j in (0, 1)], [xn[:, (2 * n + j) % 4] for j in (0, 1)],
                                  lambda i, j: i.then_inc(s_xn, 1))
                        dve.drain()

        silu_g = sb("silu_g", [P, 2, HALF * P])
        hid = sb("hid", [P, 2, HALF * P])
        hs = sb("hs", [P, 2, 2, HALF * P], F32R)
        res = sb("res", [P, HALF, D])
        pe_h, pe_o, act_g, act_h, dve_h, dve_l, dve_x, s_out = (sem(n) for n in ("pe_h", "pe_o", "act_g", "act_h", "dve_h", "dve_l", "dve_x", "out"))
        block = stack.enter_context(nc.Block())

        @block.sync
        def _(sp):
            with sp.Fori(0, 2) as k:
                for b in range(HALF):
                    sp.wait_ge(dve_x, k * HALF + (b + 2))
                    sp.dma_start(out[bass.ds(HALF * k + b, 1)].rearrange("a p d -> (a p) d"), res[:, b]).then_inc(s_out, 16)
            sp.wait_ge(s_out, 1 + 16 * 2 * HALF)

        @block.tensor
        def _(pe):
            with pe.Fori(0, 2) as k:
                tok = bass.ds(k * (HALF * P), HALF * P)

                def down(c):
                    r = rows[c]
                    pe.wait_ge(dve_l, k * NH + (c + 1))
                    for b in range(HALF):
                        i = product(pe, ps[:, 4 + b], [[hs[0:r, c % 2, a, b * P:(b + 1) * P] for a in (0, 1)]], [[w3[0:r, a, c] for a in (0, 1)]],
                                    first=c == 0, last=c == NH - 1)
                    i.then_inc(pe_o, 1)

                for c in range(NH):
                    if c >= 2:
                        pe.wait_ge(dve_h, k * NH + (c - 1))
                    cols = slice(c * P, c * P + rows[c])
                    for m, w in enumerate((w1, w2)):
                        i = product(pe, ps[0:rows[c], 2 * (c % 2) + m], [[w[:, a, kc, cols] for a in (0, 1)] for kc in range(K_CH)],
                                    [[xnT[:, a, kc, tok] for a in (0, 1)] for kc in range(K_CH)])
                    i.then_inc(pe_h, 1)
                    if c == 0:
                        pe.wait_ge(dve_x, k * HALF + 1)
                    else:
                        down(c - 1)
                down(NH - 1)

        @block.scalar
        def _(act):
            with act.Fori(0, 2) as k:
                for c in range(NH + 1):
                    if c < NH:
                        r = rows[c]
                        act.wait_ge(pe_h, k * NH + (c + 1))
                        act.activation(silu_g[0:r, c % 2], ps[0:r, 2 * (c % 2)], ACT.Silu).then_inc(act_g, 1)
                        act.wait_ge(dve_h, k * NH + (c + 1))
                        act.copy(hs[0:r, c % 2, 0], hid[0:r, c % 2]).then_inc(act_h, 1)

        @block.vector
        def _(dve):
            dve.sem_inc(dve_x, 1)
            dve.sem_inc(s_out, 1)
            with dve.Fori(0, 2) as k:
                for c in range(NH):
                    r = rows[c]
                    dve.wait_ge(act_g, k * NH + (c + 1))
                    if c >= 2:
                        dve.wait_ge(pe_o, k * NH + (c - 1))
                    dve.tensor_tensor(hid[0:r, c % 2], ps[0:r, 2 * (c % 2) + 1], silu_g[0:r, c % 2], ALU.mult).then_inc(dve_h, 1)
                    dve.wait_ge(act_h, k * NH + (c + 1))
                    dve.tensor_tensor(hs[0:r, c % 2, 1], hid[0:r, c % 2], hs[0:r, c % 2, 0], ALU.subtract).then_inc(dve_l, 1)
                dve.wait_ge(pe_o, k * NH + NH)
                for b in range(HALF):
                    dve.wait_ge(s_out, k * (16 * HALF) + 1)
                    dve.tensor_tensor(res[:, b], ps[:, 4 + b], resid[:, bass.ds(HALF * k + b, 1)].rearrange("p a d -> p (a d)"), ALU.add).then_inc(dve_x, 1)


def four_layers(nc, w, out):
    scratch = nc.dram_tensor("dequantized", w["quantized"].shape, F32, kind="Internal").ap()
    codes = (w["quantized"], scratch)
    with ExitStack() as stack:
        resid = stack.enter_context(nc.sbuf_tensor("resid", [P, N_BATCH, D], F32))
        xnT = stack.enter_context(nc.sbuf_tensor("xnT", [P, 2, K_CH, N_BATCH * P], F32R))
        correlation_and_quantized_ffn(nc, resid, xnT, w["layer0"], codes, {"dve": (0, 1)})
        with nc.sbuf_tensor("ctxT", [P, 2, K_CH, N_BATCH * P], F32R) as ctxT:
            grouped_attention(nc, "g1_", resid, xnT, ctxT, w["ctxT"], w["gqa1"], None, codes, {"dve": (4, 2), "pool": (16, 1)})
        expert_group_and_permuted_ffn(nc, resid, xnT, w["layer12"], codes, {"dve": (22, 2), "pool": (30, 1)})
        with nc.sbuf_tensor("ctxT_again", [P, 2, K_CH, N_BATCH * P], F32R) as ctxT:
            grouped_attention(nc, "g3_", resid, xnT, ctxT, w["ctxT"], w["gqa3"], w["tables3"], codes, {})
        w3 = scratch[2 * HIDDEN:3 * HIDDEN].rearrange("a b -> (a b)").rearrange("(d h) -> d h", d=D)
        swiglu(nc, resid, xnT, (scratch[0:HIDDEN], scratch[HIDDEN:2 * HIDDEN], w3), w["ident"], out)


def kernel(**inputs):
    import concourse.bacc as _bacc
    from concourse.bass_utils import run_bass_kernel_spmd as _run

    I = {name: np.asarray(a) for name, a in inputs.items()}
    tokens = N_BATCH * P
    chunks = lambda a: a.reshape(K_CH, P, -1).transpose(1, 0, 2)
    q_in = lambda a: a.reshape(K_CH, P, N_KV, GROUP, P).transpose(2, 3, 1, 0, 4)
    kv_in = lambda a: a.reshape(K_CH, P, N_KV, P).transpose(2, 1, 0, 3)
    kv_cols = N_KV * P

    inv_freq = (1.0 / np.float32(10000.0) ** (np.arange(0, HEAD_DIM, 2, dtype=np.float32) / np.float32(HEAD_DIM))).astype(np.float32)
    angle = np.arange(P, dtype=np.float32)[:, None] * inv_freq[None]
    cos, sin = np.cos(angle).T, np.sin(angle).T
    constants = {
        "ident": np.eye(P, dtype=np.float32),
        "dft": dft_matrices(),
        "iota": np.arange(D, dtype=np.float32)[None],
        "iota_col": np.arange(D, dtype=np.float32).reshape(K_CH, P).T,
        "group_ones": np.kron(np.eye(8, dtype=np.float32), np.ones((16, 16), np.float32)),
        "cosT": np.concatenate([cos, cos], 0),
        "sinT": np.concatenate([sin, -sin], 0),
        "mask": np.where(np.tril(np.ones((P, P), bool)), 0.0, -1e30).astype(np.float32),
    }
    low_rank = np.concatenate([I["L1_ffn_A_w"].reshape(P, D), I["L1_ffn_W_gate"], I["L1_ffn_W_thr"][None], np.zeros((1, D), np.float32)], 0)
    perm = I["L2_ffn_perm"]
    arrays = {
        **constants,
        "x": I["x"], "ctx": I["ctx_4096"],
        "ctxT": I["ctx_4096"].reshape(tokens, K_CH, P).transpose(2, 1, 0),
        "w8": chunks(I["L0_ffn_weight"].T), "bias8": I["L0_ffn_bias"][None],
        "wq1": q_in(I["L1_xattn_Wq"]), "wk1": kv_in(I["L1_xattn_Wkv"][:, :kv_cols]), "wv1": kv_in(I["L1_xattn_Wkv"][:, kv_cols:]),
        "wo1": I["L1_xattn_Wo"].reshape(N_KV, GROUP, P, D),
        "bq1": I["L1_xattn_bq"].reshape(-1, P).T, "bk1": I["L1_xattn_bkv"][:kv_cols].reshape(-1, P).T,
        "bv1": I["L1_xattn_bkv"][kv_cols:].reshape(-1, P).T, "bo1": I["L1_xattn_bo"][None],
        "wb": chunks(I["L1_ffn_W_base"].T).reshape(P, -1), "wl": chunks(low_rank.T).reshape(P, -1),
        "wB": I["L1_ffn_B_w"].transpose(0, 2, 1).reshape(P, D),
        "thr_b": I["L1_ffn_b_thr"].reshape(1, 1), "bias_b": I["L1_ffn_b_base"][None],
        "wp": I["L2_xattn_Wp"].T, "wg": I["L2_xattn_Wg"].T, "wt": I["L2_xattn_Wt"],
        "wz": I["L2_xattn_Wz"].reshape(8, 16, 16).transpose(0, 2, 1),
        "gn_w": I["L2_xattn_gn_w"][:, None], "gn_b": I["L2_xattn_gn_b"][:, None],
        "up": I["L2_ffn_up"].reshape(4, P, P).transpose(1, 0, 2).reshape(P, -1),
        "down": I["L2_ffn_down"].reshape(4, 4, P, 32).transpose(2, 0, 1, 3),
        "perm": perm[None], "perm_col": perm.reshape(K_CH, P).T,
        "wq3": q_in(I["L3_xattn_Wq"].T), "wk3": kv_in(I["L3_xattn_Wk"].T), "wv3": kv_in(I["L3_xattn_Wv"].T),
        "wo3": I["L3_xattn_Wd"].T.reshape(N_KV, GROUP, P, D),
        "quantized": np.concatenate([I["L3_ffn_w1"], I["L3_ffn_w2"], I["L3_ffn_w3"].reshape(HIDDEN, D),
                                     np.zeros((CODE_TILES * P - 3 * HIDDEN, D), np.float32)], 0),
    }
    nc = _bacc.Bacc("TRN2", target_bir_lowering=False, num_devices=1, dynamic_dma_scratch_size=512)
    feeds, d = {}, {}
    for name, a in arrays.items():
        a = np.ascontiguousarray(a)
        feeds[f"in_{name}_dram"] = a
        d[name] = nc.dram_tensor(f"in_{name}_dram", a.shape, mybir.dt.from_np(a.dtype), kind="ExternalInput").ap()
    out = nc.dram_tensor("out_0_dram", (N_BATCH, P, D), F32, kind="ExternalOutput").ap()
    pick = lambda *names: {n.rstrip("13"): d[n] for n in names}
    four_layers(nc, {
        "ident": d["ident"], "ctxT": d["ctxT"], "layer0": d, "layer12": d,
        "gqa1": pick("wq1", "wk1", "wv1", "wo1", "bq1", "bk1", "bv1", "bo1", "ident"),
        "gqa3": pick("wq3", "wk3", "wv3", "wo3", "ident"),
        "tables3": (d["cosT"], d["sinT"], d["mask"]),
        "quantized": d["quantized"],
    }, out)
    r = _run(nc, [feeds], core_ids=[0])
    return r.results[0]["out_0_dram"]
```
